# Optimizing a Trainium2 kernel written in Bass

```python
import numpy as np
import jax
import jax.numpy as jnp

def _softmax(x, axis=-1):
    return jax.nn.softmax(x, axis=axis)

def _gelu(x):
    return jax.nn.gelu(x, approximate=True)

def _silu(x):
    return jax.nn.silu(x)

def _sigmoid(x):
    return jax.nn.sigmoid(x)

def _layernorm(x, axis=-1, eps=1e-05):
    m = jnp.mean(x, axis=axis, keepdims=True)
    v = jnp.var(x, axis=axis, keepdims=True)
    return (x - m) / jnp.sqrt(v + eps)

def _scatter_add(tgt, idx, src, axis=0):
    return tgt.at[idx].add(src)

def _segment_sum(src, seg, n):
    return jax.ops.segment_sum(src, seg, n)
kernel_name = 'mk_adaln_ffn_d2_seqx_r8_fbfce9'

def setup_inputs(seed: int=0):
    np.random.seed(seed)
    _w = jnp.asarray

    def _rec_inputs():
        import jax
        import jax.numpy as jnp
        _rk = jax.random.key(seed)
        x = -0.000125 + 0.9999 * jax.random.normal(jax.random.fold_in(_rk, 1), (32, 32, 512), jnp.float32)
        _lenS = 32 - jax.random.randint(jax.random.fold_in(_rk, 7), (32,), 0, max(1, 32 // 4) + 1, jnp.int32)
        _lenS2 = 32 - jax.random.randint(jax.random.fold_in(_rk, 8), (32,), 0, max(1, 32 // 4) + 1, jnp.int32)
        itok_B_3_7 = jax.random.randint(jax.random.fold_in(_rk, 11), (32,), 3, 8, jnp.int32)
        itok_B_0_7 = jax.random.randint(jax.random.fold_in(_rk, 12), (32,), 0, 8, jnp.int32)
        return (x, itok_B_3_7, itok_B_0_7)
    x, itok_B_3_7, itok_B_0_7 = _rec_inputs()

    def _L0_cond_setup():
        import jax, jax.numpy as jnp
        import numpy as np
        RANK = 16
        ALPHA = 16.0
        SCALING = ALPHA / RANK
        N_ADAPTERS = 8
        IN_F = 512
        OUT_F = 512
        BATCH = 4
        SEQ = 256
        key = jax.random.key(seed)
        kx, ka, kb, ki = jax.random.split(key, 4)
        x = jax.random.normal(kx, (BATCH, SEQ, IN_F), dtype=jnp.float32)
        A = jax.random.normal(ka, (N_ADAPTERS, OUT_F, RANK), dtype=jnp.float32) * 0.02
        B = jax.random.normal(kb, (N_ADAPTERS, RANK, IN_F), dtype=jnp.float32) * 0.02
        adapter_ids = jax.random.randint(ki, (BATCH,), 0, N_ADAPTERS, dtype=jnp.int32)
        return {'x': x, 'A': A, 'B': B, 'adapter_ids': adapter_ids}
    _L0_cond_all = _L0_cond_setup()
    _L0_cond_in = {k: v for k, v in _L0_cond_all.items() if k in ('A', 'B')}
    del _L0_cond_all

    def _L0_ffn_setup():
        import jax, jax.numpy as jnp
        import numpy as np
        R = 16
        NUM_EXPERTS = 8
        TOP_K = 2
        LORA_ALPHA = 32
        SCALING = LORA_ALPHA / R
        key = jax.random.key(seed)
        ks = jax.random.split(key, 6)
        d_in, d_out = (512, 512)
        x = jax.random.normal(ks[0], (4, 256, d_in), dtype=jnp.float32)
        W_base = jax.random.normal(ks[1], (d_out, d_in), dtype=jnp.float32) * 0.02
        b_base = jax.random.normal(ks[2], (d_out,), dtype=jnp.float32) * 0.02
        W_router = jax.random.normal(ks[3], (NUM_EXPERTS, d_in), dtype=jnp.float32) * 0.01
        A = jax.random.normal(ks[4], (NUM_EXPERTS, R, d_in), dtype=jnp.float32) * 0.02
        B = jax.random.normal(ks[5], (NUM_EXPERTS, d_out, R), dtype=jnp.float32) * 0.02
        return {'x': x, 'W_base': W_base, 'b_base': b_base, 'W_router': W_router, 'A': A, 'B': B}
    _L0_ffn_all = _L0_ffn_setup()
    _L0_ffn_in = {k: v for k, v in _L0_ffn_all.items() if k in ('W_base', 'b_base', 'W_router', 'A', 'B')}
    del _L0_ffn_all

    def _L1_cond_setup():
        import jax, jax.numpy as jnp
        import numpy as np
        TOP_K = 2
        LANG_BIAS = 5.0
        SCALING = 32.0 / 16.0
        LANGUAGE_PAD_ID = -1
        key = jax.random.key(seed)
        ks = jax.random.split(key, 6)
        B, T, D, O, E, R = (4, 256, 512, 512, 8, 16)
        x = jax.random.normal(ks[0], (B, T, D), dtype=jnp.float32)
        language_ids = jax.random.randint(ks[1], (B,), 0, E).astype(jnp.int64)
        W = jax.random.normal(ks[2], (O, D), dtype=jnp.float32) * (1.0 / np.sqrt(D))
        Wr = jax.random.normal(ks[3], (E, D), dtype=jnp.float32) * (1.0 / np.sqrt(D))
        A = jax.random.normal(ks[4], (E, R, D), dtype=jnp.float32) * (1.0 / np.sqrt(D))
        Bm = jax.random.normal(ks[5], (O, R), dtype=jnp.float32) * 0.0
        Bm = jnp.broadcast_to(Bm, (E, O, R)) + jax.random.normal(ks[5], (E, O, R), dtype=jnp.float32) * 0.02
        return {'x': x, 'language_ids': language_ids, 'W': W, 'Wr': Wr, 'A': A, 'B': Bm}
    _L1_cond_all = _L1_cond_setup()
    _L1_cond_in = {k: v for k, v in _L1_cond_all.items() if k in ('W', 'Wr', 'A', 'B')}
    del _L1_cond_all

    def _L1_ffn_setup():
        import jax, jax.numpy as jnp
        import numpy as np
        LORA_R = 16
        SCALE = 16.0 / np.sqrt(16.0)
        NUM_EXPERTS = 4
        TOP_K = 2
        IN_F = 512
        OUT_F = 512
        key = jax.random.key(seed)
        k_x, k_a, k_b, k_r = jax.random.split(key, 4)
        x = jax.random.normal(k_x, (2, 256, IN_F), dtype=jnp.float32)
        A = jax.random.normal(k_a, (NUM_EXPERTS, LORA_R, IN_F), dtype=jnp.float32) * (1.0 / np.sqrt(IN_F))
        B = jax.random.normal(k_b, (NUM_EXPERTS, OUT_F, LORA_R), dtype=jnp.float32) * 0.02
        Wr = jax.random.normal(k_r, (NUM_EXPERTS, IN_F), dtype=jnp.float32) * 0.02
        return {'x': x, 'A': A, 'B': B, 'Wr': Wr}
    _L1_ffn_all = _L1_ffn_setup()
    _L1_ffn_in = {k: v for k, v in _L1_ffn_all.items() if k in ('A', 'B', 'Wr')}
    del _L1_ffn_all
    return {'x': x, 'itok_B_3_7': itok_B_3_7, 'itok_B_0_7': itok_B_0_7, 'L0_cond_A': _L0_cond_in['A'], 'L0_cond_B': _L0_cond_in['B'], 'L0_ffn_W_base': _L0_ffn_in['W_base'], 'L0_ffn_b_base': _L0_ffn_in['b_base'], 'L0_ffn_W_router': _L0_ffn_in['W_router'], 'L0_ffn_A': _L0_ffn_in['A'], 'L0_ffn_B': _L0_ffn_in['B'], 'L1_cond_W': _L1_cond_in['W'], 'L1_cond_Wr': _L1_cond_in['Wr'], 'L1_cond_A': _L1_cond_in['A'], 'L1_cond_B': _L1_cond_in['B'], 'L1_ffn_A': _L1_ffn_in['A'], 'L1_ffn_B': _L1_ffn_in['B'], 'L1_ffn_Wr': _L1_ffn_in['Wr']}

def reference(x, itok_B_3_7, itok_B_0_7, L0_cond_A, L0_cond_B, L0_ffn_W_base, L0_ffn_b_base, L0_ffn_W_router, L0_ffn_A, L0_ffn_B, L1_cond_W, L1_cond_Wr, L1_cond_A, L1_cond_B, L1_ffn_A, L1_ffn_B, L1_ffn_Wr):
    import jax
    import jax.numpy as jnp

    def _L0_cond_ref(x, A, B, adapter_ids):
        import jax, jax.numpy as jnp
        import numpy as np
        RANK = 16
        ALPHA = 16.0
        SCALING = ALPHA / RANK
        N_ADAPTERS = 8
        IN_F = 512
        OUT_F = 512
        BATCH = 4
        SEQ = 256
        B_sel = B[adapter_ids]
        A_sel = A[adapter_ids]
        Bx = jnp.einsum('bni,bri->bnr', x, B_sel)
        out = jnp.einsum('bnr,bor->bno', Bx, A_sel)
        return out * SCALING

    def _L0_ffn_ref(x, W_base, b_base, W_router, A, B):
        import jax, jax.numpy as jnp
        import numpy as np
        R = 16
        NUM_EXPERTS = 8
        TOP_K = 2
        LORA_ALPHA = 32
        SCALING = LORA_ALPHA / R
        orig_shape = x.shape
        d_in = x.shape[-1]
        x_flat = x.reshape(-1, d_in)
        logits = x_flat @ W_router.T
        probs = jax.nn.softmax(logits, axis=-1)
        topk_probs, topk_idx = jax.lax.top_k(probs, TOP_K)
        topk_probs = topk_probs / jnp.sum(topk_probs, axis=-1, keepdims=True)
        onehot = jax.nn.one_hot(topk_idx, NUM_EXPERTS, dtype=x.dtype)
        combine = jnp.einsum('nk,nke->ne', topk_probs, onehot)
        h = jnp.einsum('nd,erd->ner', x_flat, A)
        hw = h * combine[:, :, None]
        expert_out = jnp.einsum('ner,eor->no', hw, B) * SCALING
        base_out = x_flat @ W_base.T + b_base
        out = base_out + expert_out
        return out.reshape(*orig_shape[:-1], W_base.shape[0])

    def _L1_cond_ref(x, language_ids, W, Wr, A, B):
        import jax, jax.numpy as jnp
        import numpy as np
        TOP_K = 2
        LANG_BIAS = 5.0
        SCALING = 32.0 / 16.0
        LANGUAGE_PAD_ID = -1
        base = jnp.einsum('btd,od->bto', x, W)
        E = Wr.shape[0]
        logits = jnp.einsum('btd,ed->bte', x.astype(jnp.float32), Wr.astype(jnp.float32))
        expert_targets = language_ids
        valid = expert_targets >= 0
        tgt = jnp.where(valid, expert_targets, 0)
        bias = jax.nn.one_hot(tgt, E, dtype=logits.dtype) * LANG_BIAS
        bias = jnp.where(valid[:, None], bias, 0.0)
        logits = logits + bias[:, None, :]
        topw, topi = jax.lax.top_k(logits, TOP_K)
        weights = jax.nn.softmax(topw, axis=-1)
        gates = jnp.sum(jax.nn.one_hot(topi, E, dtype=weights.dtype) * weights[..., None], axis=-2)
        gates = gates.astype(x.dtype)
        h = jnp.einsum('btd,erd->bter', x, A)
        lora_out = jnp.einsum('bter,bte,eor->bto', h, gates, B)
        return base + SCALING * lora_out

    def _L1_ffn_ref(x, A, B, Wr):
        import jax, jax.numpy as jnp
        import numpy as np
        LORA_R = 16
        SCALE = 16.0 / np.sqrt(16.0)
        NUM_EXPERTS = 4
        TOP_K = 2
        IN_F = 512
        OUT_F = 512
        orig_shape = x.shape
        flat = x.reshape(-1, orig_shape[-1])
        logits = flat @ Wr.T
        topk_vals, topk_idx = jax.lax.top_k(logits, TOP_K)
        T = flat.shape[0]
        neg_inf = jnp.finfo(logits.dtype).min
        sparse = jnp.full_like(logits, neg_inf)
        rows = jnp.arange(T)[:, None]
        sparse = sparse.at[rows, topk_idx].set(topk_vals)
        gates = jax.nn.softmax(sparse, axis=-1)
        mid = jnp.einsum('tf,erf->ter', flat, A)
        all_deltas = jnp.einsum('ter,eor->teo', mid, B) * SCALE
        delta = jnp.sum(gates[:, :, None] * all_deltas, axis=1)
        return delta.reshape(*orig_shape[:-1], -1)
    x = x + _L0_ffn_ref(_L0_cond_ref(x, L0_cond_A, L0_cond_B, itok_B_3_7), L0_ffn_W_base, L0_ffn_b_base, L0_ffn_W_router, L0_ffn_A, L0_ffn_B)
    x = x + _L1_ffn_ref(_L1_cond_ref(x, itok_B_0_7, L1_cond_W, L1_cond_Wr, L1_cond_A, L1_cond_B), L1_ffn_A, L1_ffn_B, L1_ffn_Wr)
    return x

_drawn_inputs = setup_inputs


def setup_inputs(seed=0):
    import zlib

    import numpy as np

    out = dict(_drawn_inputs(seed))
    spreads = {}
    factors = {'L0_ffn_W_router': 8.0, 'L0_ffn_A': 7.113, 'L0_ffn_B': 8.0, 'L1_cond_Wr': 3.156}
    for name, (base, spread) in spreads.items():
        noise = np.random.default_rng([zlib.crc32(name.encode()), seed]).standard_normal(out[name].shape)
        drawn = base * np.exp(spread * noise) if base else spread * noise
        out[name] = jnp.asarray(drawn.astype(out[name].dtype))
    for name, factor in factors.items():
        out[name] = (out[name] * factor).astype(out[name].dtype)
    return out
```

```python
from contextlib import ExitStack

import concourse.bass as bass
from concourse import mybir

P = 128
F32 = mybir.dt.float32
I32 = mybir.dt.int32
ALU = mybir.AluOpType
ACT = mybir.ActivationFunctionType
AX_X = mybir.AxisListType.X

L0_SCALE = 32.0 / 16.0
L1_SCALE = 32.0 / 16.0
FFN_SCALE = 16.0 / 16.0 ** 0.5
LANG_BIAS = 5.0
TOP_K = 2.0


def adaln_ffn_two_layers(nc, x, ids0, ids1, c0A, c0B, f0W, f0b, f0Wr, f0A, f0B, c1W, c1Wr, c1A, c1B, f1A, f1B, f1Wr, out):
    NB, S, D = x.shape
    N = NB * S
    TILES = N // P
    GROUPS = 2
    T = TILES // GROUPS
    GT = T * P
    C = D // P
    E, R = c0B.shape[0], c0B.shape[1]
    ER = E * R
    E4 = f1A.shape[0]
    ER4 = E4 * R
    NPP = ER4 + E4
    NM1 = D + ER + E
    N0 = ER + E
    NQ = ER + E + NPP
    GB = GT // S
    TPB = 2
    assert ER == P and D == 4 * P and TPB * NQ <= 512 and T == 2 * TPB

    with ExitStack() as ctx:
        def sb(name, shape, dt=F32):
            return ctx.enter_context(nc.sbuf_tensor(name, shape, dt))

        def bank(name):
            return ctx.enter_context(nc.psum_tensor(name, [P, 512], F32))

        def sem(name):
            return ctx.enter_context(nc.semaphore(name))

        x_sb = sb("x_sb", [P, TILES, D])
        c0B_sb = sb("c0B_sb", [P, D])
        c0A_sb = sb("c0A_sb", [P, E, C, R])
        f0W_sb = sb("f0W_sb", [P, C, D])
        f0A_sb = sb("f0A_sb", [P, D])
        f0Wr_sb = sb("f0Wr_sb", [E, D])
        f0b_sb = sb("f0b_sb", [C, P])
        f0B_sb = sb("f0B_sb", [P, E, C, R])
        c1W_sb = sb("c1W_sb", [P, C, D])
        c1Wr_sb = sb("c1Wr_sb", [E, D])
        c1A_sb = sb("c1A_sb", [P, D])
        c1B_sb = sb("c1B_sb", [P, E, C, R])
        pp_sb = sb("pp_sb", [NPP, D])
        f1B_sb = sb("f1B_sb", [P, E4, C, R])
        ids0_i = sb("ids0_i", [P, NB], I32)
        ids1_i = sb("ids1_i", [NB, 1], I32)

        c0A_er = sb("c0A_er", [P, C, E, R])
        f0B_er = sb("f0B_er", [P, C, E, R])
        c1B_er = sb("c1B_er", [P, C, E, R])
        f1B_er = sb("f1B_er", [P, C, E4, R])

        ident = sb("ident", [P, P])
        batch_of_token = sb("batch_of_token", [P, NB, S])
        part_i = sb("part_i", [P, 1], I32)
        part_f = sb("part_f", [P, 1])
        expert_i = sb("expert_i", [P, E], I32)
        expert_f = sb("expert_f", [P, E])
        lower8 = sb("lower8", [P, E, E])

        ids0_f = sb("ids0_f", [P, NB])
        ids1_f = sb("ids1_f", [NB, 1])
        below = sb("below", [P, NB])
        mask0 = sb("mask0", [P, NB])
        lang_bias = sb("lang_bias", [P, E])
        c0BT = sb("c0BT", [P, C, ER])
        f0T = sb("f0T", [P, C, NM1])
        M1 = sb("M1", [P, NM1])
        f0BT = sb("f0BT", [P, D])
        bcol = sb("bcol", [P, C])
        ppT = sb("ppT", [P, C, NPP])
        Q = sb("Q", [P, C, NQ])
        c1BP = sb("c1BP", [P, NPP])
        f1BT = sb("f1BT", [ER4, D])

        xT = sb("xT", [P, C, N])
        H = sb("H", [P, N])
        logits = sb("logits", [P, T, E])
        top = sb("top", [P, T])
        shifted = sb("shifted", [P, T, E])
        expd = sb("expd", [P, T, E])
        cmp = sb("cmp", [P, T, E, E])
        before = sb("before", [P, T, E, E])
        terms8 = sb("terms8", [P, T, E, E + 1])
        terms4 = sb("terms4", [P, T, E4, E4 + 1])
        rank = sb("rank", [P, T, E])
        picked = sb("picked", [P, T, E])
        total = sb("total", [P, T])
        inv = sb("inv", [P, T])
        gates = sb("gates", [P, T, E])
        gated = [sb(f"gated{g}", [P, T, ER]) for g in range(GROUPS)]
        gatedT = [sb(f"gatedT{g}", [P, GT]) for g in range(GROUPS)]
        out_sb = sb("out_sb", [P, TILES, D])

        tA, tD, w0, w1 = bank("tA"), bank("tD"), bank("w0"), bank("w1")
        cbank = [bank(f"c{i}") for i in range(2 * GROUPS)]
        wide = [w0, w1]

        ld = {k: sem("ld_" + k) for k in ("c0B", "x0", "x1", "x2", "x3", "xg1", "c0A", "f0W", "f0A", "small", "ids",
                                          "f0B", "c1W", "c1A", "c1B", "f1B", "pp")}
        consts_made = sem("consts_made")
        repacked = sem("repacked")
        pool_step = sem("pool_step")
        setup_step = sem("setup_step")
        lang_ready = sem("lang_ready")
        forA = sem("forA")
        emptiedA = sem("emptiedA")
        forD = sem("forD")
        emptiedD = sem("emptiedD")
        h0_done = sem("h0_done")
        H_ready = sem("H_ready")
        m1_done = sem("m1_done")
        M1_wide_ready = sem("M1_wide_ready")
        M1_small_ready = sem("M1_small_ready")
        log0_done = sem("log0_done")
        qp_done = sem("qp_done")
        qp_ready = sem("qp_ready")
        bp_done = sem("bp_done")
        bp_ready = sem("bp_ready")
        shifted_ready = sem("shifted_ready")
        exp_ready = sem("exp_ready")
        gated_ready = sem("gated_ready")
        gatedT_ready = sem("gatedT_ready")
        x1T_done = sem("x1T_done")
        x1T_ready = sem("x1T_ready")
        log1_done = sem("log1_done")
        mid_done = sem("mid_done")
        y_done = sem("y_done")
        y_out = sem("y_out")
        stored = sem("stored")
        dve_step = sem("dve_step")

        x_tok = x.rearrange("b s d -> (b s) d").rearrange("(i p) d -> p i d", p=P)
        out_tok = out.rearrange("b s d -> (b s) d").rearrange("(i p) d -> p i d", p=P)

        def er_rows(w):
            return w.rearrange("e r d -> (e r) d")

        def four_rows(w):
            return w.rearrange("e (p j) r -> p e (j r)", j=C)

        def o4(ap):
            return ap.rearrange("q (p j) -> q j p", j=C)

        ident_v = ident[:, :]

        block = ctx.enter_context(nc.Block())

        @block.sync
        def _(sp):
            sp.dma_start(c0B_sb[:, :], er_rows(c0B)).then_inc(ld["c0B"], 16)
            for i in range(T):
                sp.dma_start(x_sb[:, i, :], x_tok[:, i, :]).then_inc(ld[f"x{i}"], 16)
            sp.dma_start(c0A_sb[:, :, :, :].rearrange("p e j r -> p e (j r)"), four_rows(c0A)).then_inc(ld["c0A"], 16)
            sp.dma_start(x_sb[:, T:TILES, :], x_tok[:, T:TILES, :]).then_inc(ld["xg1"], 16)
            sp.dma_start(f0B_sb[:, :, :, :].rearrange("p e j r -> p e (j r)"), four_rows(f0B)).then_inc(ld["f0B"], 16)
            sp.dma_start(c1W_sb[:, :, :], c1W.rearrange("(p j) d -> p j d", j=C)).then_inc(ld["c1W"], 16)
            sp.dma_start(c1B_sb[:, :, :, :].rearrange("p e j r -> p e (j r)"), four_rows(c1B)).then_inc(ld["c1B"], 16)
            sp.dma_start(f1B_sb[:, :, :, :].rearrange("p e j r -> p e (j r)"), four_rows(f1B)).then_inc(ld["f1B"], 16)
            for i in range(TILES):
                sp.wait_ge(y_out, i + 1)
                sp.dma_start(out_tok[:, i, :], out_sb[:, i, :]).then_inc(stored, 16)
            sp.wait_ge(stored, 16 * TILES)

        @block.gpsimd
        def _(pool):
            nc.gpsimd.memset(ident[:, :], 0.0).then_inc(pool_step, 1)
            pool.wait_ge(pool_step, 1)
            nc.gpsimd.affine_select(out=ident[:, :], in_=ident[:, :], compare_op=ALU.not_equal, fill=1.0, base=0,
                                    pattern=[[-1, P]], channel_multiplier=1).then_inc(consts_made, 1)
            nc.gpsimd.iota(part_i[:, :], pattern=[[0, 1]], base=0, channel_multiplier=1).then_inc(consts_made, 1)
            nc.gpsimd.iota(expert_i[:, :], pattern=[[1, E]], base=0, channel_multiplier=0).then_inc(consts_made, 1)
            nc.gpsimd.memset(lower8[:, :, :], 1.0).then_inc(pool_step, 1)
            pool.wait_ge(pool_step, 2)
            nc.gpsimd.affine_select(out=lower8[:, :, :], in_=lower8[:, :, :], compare_op=ALU.is_gt, fill=0.0, base=0,
                                    pattern=[[1, E], [-1, E]], channel_multiplier=0).then_inc(consts_made, 1)
            for e in range(E):
                nc.gpsimd.memset(terms8[:, :, e, E:E + 1], float(E - 1 - e))
            for e in range(E4):
                last = nc.gpsimd.memset(terms4[:, :, e, E4:E4 + 1], float(E4 - 1 - e))
            last.then_inc(consts_made, 1)
            nc.gpsimd.memset(batch_of_token[:, :, :], 0.0).then_inc(pool_step, 1)
            pool.wait_ge(pool_step, 3)
            nc.gpsimd.affine_select(out=batch_of_token[:, :, :], in_=batch_of_token[:, :, :], compare_op=ALU.not_equal,
                                    fill=1.0, base=0, pattern=[[-1, NB], [0, S]],
                                    channel_multiplier=1).then_inc(consts_made, 1)
            for k, src, dst in (("c0A", c0A_sb, c0A_er), ("f0B", f0B_sb, f0B_er), ("c1B", c1B_sb, c1B_er),
                                ("f1B", f1B_sb, f1B_er)):
                pool.wait_ge(ld[k], 16)
                nc.gpsimd.tensor_copy(dst[:, :, :, :], src[:, :, :, :].rearrange("p e j r -> p j e r")).then_inc(repacked, 1)

        @block.scalar
        def _(act):
            act.dma_start(ids0_i[:, :], ids0.rearrange("(a b) -> a b", a=1).to_broadcast([P, NB])).then_inc(ld["ids"], 16)
            act.dma_start(ids1_i[:, :], ids1.rearrange("(b a) -> b a", a=1)).then_inc(ld["ids"], 16)
            act.dma_start(f0W_sb[:, :, :], f0W.rearrange("(k p) d -> p k d", p=P)).then_inc(ld["f0W"], 16)
            act.dma_start(f0A_sb[:, :], er_rows(f0A)).then_inc(ld["f0A"], 16)
            act.dma_start(f0Wr_sb[:, :], f0Wr).then_inc(ld["small"], 16)
            act.dma_start(c1Wr_sb[:, :], c1Wr).then_inc(ld["small"], 16)
            act.dma_start(f0b_sb[:, :], f0b.rearrange("(c p) -> c p", p=P)).then_inc(ld["small"], 16)
            act.dma_start(pp_sb[0:ER4, :], er_rows(f1A)).then_inc(ld["pp"], 16)
            act.dma_start(pp_sb[ER4:NPP, :], f1Wr).then_inc(ld["pp"], 16)
            act.dma_start(c1A_sb[:, :], er_rows(c1A)).then_inc(ld["c1A"], 16)

            seen = [0]

            def filled():
                seen[0] += 1
                act.wait_ge(forA, seen[0])

            def exps(n, e):
                act.wait_ge(shifted_ready, n)
                nc.scalar.activation(expd[:, :, 0:e], shifted[:, :, 0:e], ACT.Exp).then_inc(exp_ready, 1)

            def tview(cols, n):
                return tA[:, 0:cols * n].rearrange("p (c n) -> p c n", n=n)

            def x_tile(i):
                filled()
                nc.scalar.copy(xT[:, :, i * P:(i + 1) * P], tview(C, P)).then_inc(emptiedA, 1)

            def gated_T(g, rows):
                filled()
                nc.scalar.copy(gatedT[g][0:rows, :], tA[0:rows, :]).then_inc(emptiedA, 1)

            filled()
            nc.scalar.copy(c0BT[:, :, :], tview(C, ER)).then_inc(emptiedA, 1)
            x_tile(1)
            x_tile(3)
            for j in (1, 3):
                filled()
                nc.scalar.copy(f0T[:, j, 0:D], tA[:, :]).then_inc(emptiedA, 1)
            filled()
            nc.scalar.copy(f0T[:, :, D + ER:NM1], tview(C, E))
            nc.scalar.copy(Q[:, :, ER:ER + E], tA[:, C * E:2 * C * E].rearrange("p (c n) -> p c n", n=E))
            nc.scalar.copy(bcol[:, :], tA[:, 2 * C * E:2 * C * E + C])
            at = 2 * C * E + C
            nc.scalar.copy(ppT[:, :, :], tA[:, at:at + C * NPP].rearrange("p (c n) -> p c n", n=NPP)).then_inc(emptiedA, 1)
            act.wait_ge(m1_done, 1)
            nc.scalar.copy(M1[:, D:NM1], cbank[3][:, 0:N0]).then_inc(M1_small_ready, 1)
            x_tile(5)
            x_tile(7)
            filled()
            nc.scalar.copy(Q[:, :, 0:ER], tview(C, ER)).then_inc(emptiedA, 1)
            exps(1, E)
            filled()
            nc.scalar.activation(o4(f0BT[:, :]), tview(C, P), ACT.Copy, scale=L0_SCALE).then_inc(emptiedA, 1)
            filled()
            nc.scalar.activation(o4(f1BT[:, :]), tA[0:ER4, :].rearrange("p (c n) -> p c n", n=P), ACT.Copy,
                                 scale=FFN_SCALE).then_inc(emptiedA, 1)
            gated_T(0, ER)
            act.wait_ge(qp_done, 1)
            nc.scalar.copy(Q[:, :, ER + E:NQ], w1[:, 0:C * NPP].rearrange("p (c n) -> p c n", n=NPP)).then_inc(qp_ready, 1)
            act.wait_ge(bp_done, 1)
            nc.scalar.activation(c1BP[:, :], w0[:, 0:NPP], ACT.Copy, scale=L1_SCALE).then_inc(bp_ready, 1)
            exps(2, E)
            gated_T(1, ER)
            exps(3, E)
            gated_T(0, ER)
            exps(4, E4)
            gated_T(0, ER4)
            exps(5, E)

            def emit(i):
                act.wait_ge(y_done, i + 1)
                nc.scalar.copy(out_sb[:, i, :], wide[i % 2][:, :]).then_inc(y_out, 1)

            for i in range(T):
                emit(i)
            gated_T(1, ER)
            exps(6, E4)
            gated_T(1, ER4)
            for i in range(T, TILES):
                emit(i)

        @block.vector
        def _(dve):
            steps = [0]

            def step(ins):
                steps[0] += 1
                ins.then_inc(dve_step, 1)
                dve.wait_ge(dve_step, steps[0])

            seen = [0]

            def filled():
                seen[0] += 1
                dve.wait_ge(forD, seen[0])

            def x_tile(i):
                filled()
                nc.vector.tensor_copy(xT[:, :, i * P:(i + 1) * P],
                                      tD[:, :].rearrange("p (c n) -> p c n", n=P)).then_inc(emptiedD, 1)

            nc.vector.memset(lang_bias[:, :], 0.0).then_inc(setup_step, 1)
            dve.wait_ge(consts_made, 3)
            dve.wait_ge(ld["ids"], 32)
            nc.vector.tensor_copy(part_f[:, :], part_i[:, :]).then_inc(setup_step, 1)
            nc.vector.tensor_copy(expert_f[:, :], expert_i[:, :]).then_inc(setup_step, 1)
            nc.vector.tensor_copy(ids0_f[:, :], ids0_i[:, :]).then_inc(setup_step, 1)
            nc.vector.tensor_copy(ids1_f[:, :], ids1_i[:, :]).then_inc(setup_step, 1)
            dve.wait_ge(setup_step, 5)
            nc.vector.tensor_scalar(mask0[:, :], ids0_f[:, :], -float(R), part_f[:, 0:1], ALU.mult,
                                    ALU.add).then_inc(setup_step, 1)
            nc.vector.tensor_scalar(lang_bias[0:NB, :], expert_f[0:NB, :], ids1_f[:, 0:1], LANG_BIAS, ALU.is_equal,
                                    ALU.mult).then_inc(lang_ready, 1)
            dve.wait_ge(setup_step, 6)
            nc.vector.tensor_single_scalar(below[:, :], mask0[:, :], float(R) - 0.5, op=ALU.is_lt).then_inc(setup_step, 1)
            dve.wait_ge(setup_step, 7)
            nc.vector.scalar_tensor_tensor(out=mask0[:, :], in0=mask0[:, :], scalar=-0.5, in1=below[:, :], op0=ALU.is_gt,
                                           op1=ALU.mult).then_inc(setup_step, 1)

            def H_group(g):
                if g == 0:
                    dve.wait_ge(setup_step, 8)
                dve.wait_ge(h0_done, g + 1)
                m = mask0[:, g * GB:(g + 1) * GB].unsqueeze(2).to_broadcast([P, GB, S])
                nc.vector.tensor_tensor(H[:, g * GT:(g + 1) * GT].rearrange("p (b s) -> p b s", s=S),
                                        w0[:, :].rearrange("p (b s) -> p b s", s=S), m, ALU.mult).then_inc(H_ready, 1)

            def gate(g, e_count, log_at, h_at, terms):
                e = e_count
                n = T * e
                lg = logits[:, :, 0:e]
                for k in range(T // TPB):
                    b = cbank[2 * g + k]
                    w = h_at[1]
                    last = nc.vector.tensor_copy(logits[:, k * TPB:(k + 1) * TPB, 0:e],
                                                 b[:, 0:TPB * w].rearrange("p (t n) -> p t n", n=w)[:, :, log_at:log_at + e])
                step(last)
                nc.vector.tensor_reduce(top[:, :], lg, axis=AX_X, op=ALU.max).then_inc(dve_step, 1)
                steps[0] += 1
                cm = cmp[:, :, 0:e, 0:e]
                bf = before[:, :, 0:e, 0:e]
                nc.vector.tensor_tensor(cm, lg.unsqueeze(2).to_broadcast([P, T, e, e]),
                                        lg.unsqueeze(3).to_broadcast([P, T, e, e]), ALU.is_ge).then_inc(dve_step, 1)
                steps[0] += 1
                dve.wait_ge(dve_step, steps[0] - 1)
                nc.vector.tensor_tensor(shifted[:, :, 0:e], lg, top[:, :].unsqueeze(2).to_broadcast([P, T, e]),
                                        ALU.subtract).then_inc(shifted_ready, 1)
                dve.wait_ge(dve_step, steps[0])
                step(nc.vector.tensor_tensor(bf, cm, lower8[:, 0:e, 0:e].unsqueeze(1).to_broadcast([P, T, e, e]), ALU.mult))
                step(nc.vector.tensor_tensor(terms[:, :, :, 0:e], bf, bf.rearrange("p t a b -> p t b a"), ALU.subtract))
                step(nc.vector.tensor_reduce(rank[:, :, 0:e], terms[:, :, :, :], axis=AX_X, op=ALU.add))
                gates_done[0] += 1
                dve.wait_ge(exp_ready, gates_done[0])
                step(nc.vector.scalar_tensor_tensor(out=picked[:, :, 0:e], in0=rank[:, :, 0:e], scalar=TOP_K,
                                                    in1=expd[:, :, 0:e], op0=ALU.is_lt, op1=ALU.mult))
                step(nc.vector.reduce_sum(total[:, :], picked[:, :, 0:e], axis=AX_X))
                step(nc.vector.reciprocal(inv[:, :], total[:, :]))
                step(nc.vector.tensor_tensor(gates[:, :, 0:e], picked[:, :, 0:e],
                                             inv[:, :].unsqueeze(2).to_broadcast([P, T, e]), ALU.mult))
                for k in range(T // TPB):
                    b = cbank[2 * g + k]
                    o, w = h_at
                    h = b[:, 0:TPB * w].rearrange("p (t n) -> p t n", n=w)[:, :, o:o + e * R]
                    last = nc.vector.tensor_tensor(
                        gated[g][:, k * TPB:(k + 1) * TPB, 0:e * R].rearrange("p t (e r) -> p t e r", r=R),
                        h.rearrange("p t (e r) -> p t e r", r=R),
                        gates[:, k * TPB:(k + 1) * TPB, 0:e].unsqueeze(3).to_broadcast([P, TPB, e, R]), ALU.mult)
                last.then_inc(gated_ready, 1)

            gates_done = [0]

            def x1T_group(g):
                for j in range(C):
                    n = g * C + j
                    dve.wait_ge(x1T_done, n + 1)
                    t = xT[:, j, g * GT:(g + 1) * GT]
                    nc.vector.scalar_tensor_tensor(out=t, in0=wide[j % 2][:, :], scalar=bcol[:, j:j + 1], in1=t,
                                                   op0=ALU.add, op1=ALU.add).then_inc(x1T_ready, 1)

            x_tile(0)
            x_tile(2)
            H_group(0)
            for j in (0, 2):
                filled()
                nc.vector.tensor_copy(f0T[:, j, 0:D], tD[:, :]).then_inc(emptiedD, 1)
            filled()
            nc.vector.tensor_copy(f0T[:, :, D:D + ER], tD[:, :].rearrange("p (c n) -> p c n", n=ER)).then_inc(emptiedD, 1)
            dve.wait_ge(m1_done, 1)
            nc.vector.tensor_copy(M1[:, 0:D], w1[:, :]).then_inc(M1_wide_ready, 1)
            x_tile(4)
            x_tile(6)
            dve.wait_ge(consts_made, 5)
            dve.wait_ge(log0_done, 1)
            gate(0, E, ER, (0, N0), terms8)
            H_group(1)
            dve.wait_ge(log0_done, 2)
            gate(1, E, ER, (0, N0), terms8)
            dve.wait_ge(emptiedA, 6)
            x1T_group(0)
            dve.wait_ge(log1_done, 1)
            gate(0, E, ER, (0, NQ), terms8)
            x1T_group(1)
            dve.wait_ge(mid_done, 1)
            gate(0, E4, ER + E + ER4, (ER + E, NQ), terms4)
            dve.wait_ge(log1_done, 2)
            gate(1, E, ER, (0, NQ), terms8)
            dve.wait_ge(mid_done, 2)
            gate(1, E4, ER + E + ER4, (ER + E, NQ), terms4)

        @block.tensor
        def _(pe):
            usedA = [0]
            usedD = [0]

            def bankA():
                if usedA[0]:
                    pe.wait_ge(emptiedA, usedA[0])
                usedA[0] += 1
                return tA

            def bankD():
                if usedD[0]:
                    pe.wait_ge(emptiedD, usedD[0])
                usedD[0] += 1
                return tD

            def four(dst, src):
                for c in range(C):
                    s = src(c)
                    k = s.shape[0]
                    m = s.shape[1]
                    last = nc.tensor.transpose(dst[0:m, c * k:(c + 1) * k], s, ident[0:k, 0:k])
                return last

            def x_tile(i):
                b, s = (bankA(), forA) if i % 2 else (bankD(), forD)
                four(b, lambda c: x_sb[:, i, c * P:(c + 1) * P]).then_inc(s, 1)

            def h0(g):
                for c in range(C):
                    last = nc.tensor.matmul(w0[:, :], c0BT[:, c, :], xT[:, c, g * GT:(g + 1) * GT], start=(c == 0),
                                            stop=(c == C - 1))
                last.then_inc(h0_done, 1)

            def log0(g):
                for t in range(T):
                    b = cbank[2 * g + t // TPB]
                    o = (t % TPB) * N0
                    i = g * T + t
                    last = nc.tensor.matmul(b[:, o:o + N0], H[:, i * P:(i + 1) * P], M1[:, D:NM1], start=True, stop=True,
                                            skip_group_check=True)
                last.then_inc(log0_done, 1)

            def gated_T(g, rows, n):
                pe.wait_ge(gated_ready, n)
                four(bankA(), lambda t: gated[g][:, t, 0:rows]).then_inc(forA, 1)

            def x1T(g):
                for j in range(C):
                    n = g * C + j
                    if n >= 2:
                        pe.wait_ge(x1T_ready, n - 1)
                    b = wide[j % 2]
                    nc.tensor.matmul(b[:, :], M1[:, j * P:(j + 1) * P], H[:, g * GT:(g + 1) * GT], start=True, stop=False)
                    nc.tensor.matmul(b[:, :], f0BT[:, j * P:(j + 1) * P], gatedT[g][:, :], start=False,
                                     stop=True).then_inc(x1T_done, 1)

            def log1(g):
                pe.wait_ge(x1T_ready, (g + 1) * C)
                for t in range(T):
                    b = cbank[2 * g + t // TPB]
                    o = (t % TPB) * NQ
                    i = g * T + t
                    for c in range(C):
                        nc.tensor.matmul(b[:, o:o + NQ], xT[:, c, i * P:(i + 1) * P], Q[:, c, :],
                                         start=(c == 0 and t % TPB == 0), stop=False, skip_group_check=True)
                    last = nc.tensor.matmul(b[:, o + ER:o + ER + E],
                                            batch_of_token[:, i * (P // S):(i + 1) * (P // S), :].rearrange("p b s -> p (b s)"),
                                            lang_bias[:, :], start=False, stop=True, skip_group_check=True)
                last.then_inc(log1_done, 1)

            def mid(g):
                for t in range(T):
                    b = cbank[2 * g + t // TPB]
                    o = (t % TPB) * NQ + ER + E
                    last = nc.tensor.matmul(b[:, o:o + NPP], gatedT[g][:, t * P:(t + 1) * P], c1BP[:, :], start=False,
                                            stop=True, skip_group_check=True)
                last.then_inc(mid_done, 1)

            def y(g):
                for t in range(T):
                    i = g * T + t
                    b = wide[i % 2]
                    if i >= 2:
                        pe.wait_ge(y_out, i - 1)
                    for c in range(C):
                        nc.tensor.matmul(b[:, c * P:(c + 1) * P], xT[:, c, i * P:(i + 1) * P], ident[:, :], is_transpose=True,
                                         start=(c == 0), stop=False, skip_group_check=True)
                    nc.tensor.matmul(b[:, :], gatedT[g][0:ER4, t * P:(t + 1) * P], f1BT[:, :], start=False, stop=True,
                                     skip_group_check=True).then_inc(y_done, 1)

            pe.wait_ge(consts_made, 1)
            pe.wait_ge(ld["c0B"], 16)
            four(bankA(), lambda c: c0B_sb[:, c * P:(c + 1) * P]).then_inc(forA, 1)
            for i in range(T):
                pe.wait_ge(ld[f"x{i}"], 16)
                x_tile(i)
            pe.wait_ge(emptiedA, 3)
            pe.wait_ge(emptiedD, 2)
            h0(0)
            pe.wait_ge(ld["f0W"], 16)
            for j in range(C):
                b, s = (bankA(), forA) if j % 2 else (bankD(), forD)
                four(b, lambda k: o4(f0W_sb[:, k, :])[:, j, :]).then_inc(s, 1)
            pe.wait_ge(ld["f0A"], 16)
            four(bankD(), lambda j: o4(f0A_sb[:, :])[:, j, :]).then_inc(forD, 1)
            pe.wait_ge(ld["small"], 48)
            pe.wait_ge(ld["pp"], 32)
            b = bankA()
            four(b[:, 0:C * E], lambda j: o4(f0Wr_sb[:, :])[:, j, :])
            four(b[:, C * E:2 * C * E], lambda c: c1Wr_sb[:, c * P:(c + 1) * P])
            at = 2 * C * E
            nc.tensor.transpose(b[:, at:at + C], f0b_sb[:, :], ident[0:C, 0:C])
            at += C
            four(b[:, at:at + C * NPP], lambda j: o4(pp_sb[:, :])[:, j, :]).then_inc(forA, 1)
            pe.wait_ge(repacked, 1)
            pe.wait_ge(emptiedA, 6)
            pe.wait_ge(emptiedD, 5)
            for j in range(C):
                a = c0A_er[:, j, :, :].rearrange("p e r -> p (e r)")
                nc.tensor.matmul(cbank[3][:, 0:N0], a, f0T[:, j, D:NM1], start=(j == 0), stop=(j == C - 1))
                last = nc.tensor.matmul(w1[:, :], a, f0T[:, j, 0:D], start=(j == 0), stop=(j == C - 1))
            last.then_inc(m1_done, 1)
            pe.wait_ge(ld["xg1"], 16)
            for i in range(T, TILES):
                x_tile(i)
            pe.wait_ge(H_ready, 1)
            pe.wait_ge(M1_small_ready, 1)
            log0(0)
            pe.wait_ge(emptiedA, 8)
            pe.wait_ge(emptiedD, 7)
            h0(1)
            pe.wait_ge(ld["c1A"], 16)
            four(bankA(), lambda c: c1A_sb[:, c * P:(c + 1) * P]).then_inc(forA, 1)
            pe.wait_ge(ld["c1W"], 16)
            pe.wait_ge(M1_wide_ready, 1)
            for c in range(C):
                for j in range(C):
                    last = nc.tensor.matmul(w1[:, c * NPP:(c + 1) * NPP], c1W_sb[:, j, c * P:(c + 1) * P], ppT[:, j, :],
                                            start=(j == 0), stop=(j == C - 1), skip_group_check=True)
            last.then_inc(qp_done, 1)
            pe.wait_ge(H_ready, 2)
            log0(1)
            pe.wait_ge(repacked, 3)
            for j in range(C):
                last = nc.tensor.matmul(w0[:, 0:NPP], c1B_er[:, j, :, :].rearrange("p e r -> p (e r)"), ppT[:, j, :], start=(j == 0), stop=(j == C - 1))
            last.then_inc(bp_done, 1)
            pe.wait_ge(repacked, 2)
            four(bankA(), lambda j: f0B_er[:, j, :, :].rearrange("p e r -> p (e r)")).then_inc(forA, 1)
            pe.wait_ge(repacked, 4)
            pe.wait_ge(consts_made, 6)
            four(bankA(), lambda j: f1B_er[:, j, :, :].rearrange("p e r -> p (e r)")).then_inc(forA, 1)

            gated_T(0, ER, 1)
            pe.wait_ge(qp_ready, 1)
            pe.wait_ge(bp_ready, 1)
            pe.wait_ge(emptiedA, 12)
            x1T(0)
            log1(0)
            gated_T(1, ER, 2)
            pe.wait_ge(emptiedA, 13)
            x1T(1)
            gated_T(0, ER, 3)
            pe.wait_ge(emptiedA, 14)
            mid(0)
            log1(1)
            gated_T(0, ER4, 4)
            pe.wait_ge(emptiedA, 15)
            y(0)
            gated_T(1, ER, 5)
            pe.wait_ge(emptiedA, 16)
            mid(1)
            gated_T(1, ER4, 6)
            pe.wait_ge(emptiedA, 17)
            y(1)


_INS = ['x', 'itok_B_3_7', 'itok_B_0_7', 'L0_cond_A', 'L0_cond_B', 'L0_ffn_W_base', 'L0_ffn_b_base', 'L0_ffn_W_router',
        'L0_ffn_A', 'L0_ffn_B', 'L1_cond_W', 'L1_cond_Wr', 'L1_cond_A', 'L1_cond_B', 'L1_ffn_A', 'L1_ffn_B', 'L1_ffn_Wr']
_OUTS = [((32, 32, 512), 'float32')]


def kernel(**inputs):
    import numpy as _np
    import concourse.bacc as _bacc
    from concourse import mybir as _mybir
    from concourse.bass_utils import run_bass_kernel_spmd as _run

    nc = _bacc.Bacc("TRN2", target_bir_lowering=False, num_devices=1)
    arrays, args = {}, []
    for name in _INS:
        a = _np.ascontiguousarray(inputs[name])
        arrays[f"in_{name}_dram"] = a
        args.append(nc.dram_tensor(f"in_{name}_dram", a.shape, _mybir.dt.from_np(a.dtype), kind="ExternalInput").ap())
    for i, (shape, dtype) in enumerate(_OUTS):
        dt = _mybir.dt.from_np(_np.dtype(dtype))
        args.append(nc.dram_tensor(f"out_{i}_dram", shape, dt, kind="ExternalOutput").ap())
    adaln_ffn_two_layers(nc, *args)
    r = _run(nc, [arrays], core_ids=[0])
    got = tuple(r.results[0][f"out_{i}_dram"] for i in range(len(_OUTS)))
    return got[0]
```

```python
from contextlib import ExitStack

import concourse.bass as bass
from concourse import mybir

P = 128
F32 = mybir.dt.float32
I32 = mybir.dt.int32
F32R = mybir.dt.float32r
BF16 = mybir.dt.bfloat16
ALU = mybir.AluOpType
ACT = mybir.ActivationFunctionType
AX_X = mybir.AxisListType.X

L0_SCALE = 32.0 / 16.0
L1_SCALE = 32.0 / 16.0
FFN_SCALE = 16.0 / 16.0 ** 0.5
LANG_BIAS = 5.0
TOP_K = 2.0


def adaln_ffn_two_layers(nc, x, ids0, ids1, c0A, c0B, f0W, f0b, f0Wr, f0A, f0B, c1W, c1Wr, c1A, c1B, f1A, f1B, f1Wr, out):
    NB, S, D = x.shape
    N = NB * S
    TILES = N // P
    HALF = TILES // 2
    C = D // P
    E, R = c0B.shape[0], c0B.shape[1]
    ER = E * R
    E4 = f1A.shape[0]
    ER4 = E4 * R
    NPP = ER4 + E4
    NM1 = D + ER + E
    N0 = ER + E
    NQ = ER + E + NPP
    TPB = 2
    GROUPS = [range(0, 4), range(4, 6), range(6, 8)]
    HALVES = [range(0, HALF), range(HALF, TILES)]
    assert ER == P and 2 * ER4 == P and D == 4 * P and TPB * NQ <= 512 and TILES == 8

    WARM = [8, 3, 0]

    FILLS = ["c0B", "x0", "x1", "x2", "x3", "fW0", "fW1", "fW2", "fW3", "f0A", "small", "x4", "x5", "x6", "x7",
             "f0B", "a0", "c1A", "f1B", "a1", "b0", "m0", "b1", "b2", "m1", "m2"]
    COPIED = ["fW0", "fW1", "fW2", "fW3", "f0A", "small", "f0B", "c1A", "f1B", "b0", "b1", "b2"]
    SPLITS = ["c0B", "x0", "x1", "x2", "x3", "H0", "M1", "x4", "x5", "x6", "x7", "f0B", "a0", "H1", "f1B", "a1", "m0",
              "m1", "m2"]

    with ExitStack() as ctx:
        def sb(name, shape, dt=F32):
            return ctx.enter_context(nc.sbuf_tensor(name, shape, dt))

        def bank(name):
            return ctx.enter_context(nc.psum_tensor(name, [P, 512], F32))

        def sem(name):
            return ctx.enter_context(nc.semaphore(name))

        def pair(name, shape):
            return sb(name + "_hi", shape, F32R), sb(name + "_lo", shape, F32R)

        x_sb = sb("x_sb", [P, TILES, D])
        c0B_sb = sb("c0B_sb", [P, D])
        c0A_sb = sb("c0A_sb", [P, E, C, R])
        f0W_sb = sb("f0W_sb", [P, C, D])
        f0A_sb = sb("f0A_sb", [P, D])
        f0Wr_sb = sb("f0Wr_sb", [E, D])
        f0b_sb = sb("f0b_sb", [C, P])
        f0B_sb = sb("f0B_sb", [P, E, C, R])
        c1W_sb = sb("c1W_sb", [P, C, D])
        c1Wr_sb = sb("c1Wr_sb", [E, D])
        c1A_sb = sb("c1A_sb", [P, D])
        c1B_sb = sb("c1B_sb", [P, E, C, R])
        pp_sb = sb("pp_sb", [NPP, D])
        f1B_sb = sb("f1B_sb", [P, E4, C, R])
        ids0_i = sb("ids0_i", [P, NB], I32)
        ids1_i = sb("ids1_i", [NB, 1], I32)

        c0A_er = sb("c0A_er", [P, C, E, R])
        f0B_er = sb("f0B_er", [P, C, E, R])
        c1B_er = sb("c1B_er", [P, C, E, R])
        f1B_er = sb("f1B_er", [P, C, E4, R])

        ident = sb("ident", [P, P])
        batch_of_token = sb("batch_of_token", [P, NB, S], BF16)
        part_i = sb("part_i", [P, 1], I32)
        part_f = sb("part_f", [P, 1])
        expert_i = sb("expert_i", [P, E], I32)
        expert_f = sb("expert_f", [P, E])
        lower8 = sb("lower8", [P, E, E], BF16)

        ids0_f = sb("ids0_f", [P, NB])
        ids1_f = sb("ids1_f", [NB, 1])
        below = sb("below", [P, NB])
        mask0 = sb("mask0", [P, NB])
        lang_bias = sb("lang_bias", [P, E], BF16)
        c0BT = pair("c0BT", [P, C, ER])
        f0T = sb("f0T", [P, C, NM1])
        M1 = pair("M1", [P, D])
        M1_narrow = sb("M1_narrow", [P, N0])
        f0BT = pair("f0BT", [P, D])
        bcol = sb("bcol", [P, C])
        ppT = sb("ppT", [P, C, NPP])
        Q = sb("Q", [P, C, NQ])
        c1BP = sb("c1BP", [P, NPP])
        f1BT_hi2 = sb("f1BT_hi2", [P, D], F32R)
        f1BT_lo = sb("f1BT_lo", [ER4, D], F32R)
        f0BT_full = sb("f0BT_full", [P, D])
        f1BT_full = sb("f1BT_full", [ER4, D])

        xT = sb("xT", [P, C, N])
        xTs = pair("xTs", [P, C, N])
        H_full = sb("H_full", [P, N])
        H = pair("H", [P, N])
        logits = sb("logits", [P, HALF, E])
        top = sb("top", [P, HALF])
        shifted = sb("shifted", [P, HALF, E])
        expd = sb("expd", [P, HALF, E])
        cmp = sb("cmp", [P, HALF, E, E], BF16)
        before = sb("before", [P, HALF, E, E], BF16)
        terms8 = sb("terms8", [P, HALF, E, E + 1], BF16)
        terms4 = sb("terms4", [P, HALF, E4, E4 + 1], BF16)
        rank = sb("rank", [P, HALF, E])
        picked = sb("picked", [P, HALF, E])
        total = sb("total", [P, HALF])
        inv = sb("inv", [P, HALF])
        gates = sb("gates", [P, HALF, E])
        gated = sb("gated", [P, TILES, ER])
        gatedT = pair("gatedT", [P, N])
        gatedT1 = sb("gatedT1", [P, N])
        mixedT = sb("mixedT", [P, N], F32R)
        out_sb = sb("out_sb", [P, TILES, D])

        tbank = [bank("t0"), bank("t1")]
        wide = [bank("w0"), bank("w1")]
        cbank = [bank(f"c{i}") for i in range(TILES // TPB)]

        ld = {k: sem("ld_" + k) for k in ("c0B", "x01", "x23", "xh1", "c0A", "f0W", "f0A", "small", "router", "ids",
                                          "f0B", "c1W", "c1A", "c1B", "f1B", "pp")}
        filled = [sem("filled0"), sem("filled1")]
        emptied = [sem("emptied0"), sem("emptied1")]
        hi_ready = sem("hi_ready")
        lo_ready = sem("lo_ready")
        consts_made = sem("consts_made")
        repacked = sem("repacked")
        pool_step = sem("pool_step")
        setup_step = sem("setup_step")
        lang_ready = sem("lang_ready")
        h0_done = sem("h0_done")
        H_ready = sem("H_ready")
        m1_wide_done = sem("m1_wide_done")
        m1_narrow_done = sem("m1_narrow_done")
        log0_done = sem("log0_done")
        narrow_ready = sem("narrow_ready")
        qp_done = sem("qp_done")
        qp_ready = sem("qp_ready")
        bp_done = sem("bp_done")
        bp_ready = sem("bp_ready")
        xT_ready = sem("xT_ready")
        shifted_ready = sem("shifted_ready")
        exp_ready = sem("exp_ready")
        gated_ready = sem("gated_ready")
        x1T_done = sem("x1T_done")
        x1T_ready = sem("x1T_ready")
        log1_done = sem("log1_done")
        mid_done = sem("mid_done")
        y_done = sem("y_done")
        y_out = sem("y_out")
        last_y_out = sem("last_y_out")
        stored = sem("stored")
        dve_step = sem("dve_step")

        x_tok = x.rearrange("b s d -> (b s) d").rearrange("(i p) d -> p i d", p=P)
        out_tok = out.rearrange("b s d -> (b s) d").rearrange("(i p) d -> p i d", p=P)

        def er_rows(w):
            return w.rearrange("e r d -> (e r) d")

        def four_rows(w):
            return w.rearrange("e (p j) r -> p e (j r)", j=C)

        def o4(ap):
            return ap.rearrange("q (p j) -> q j p", j=C)

        def fill_bank(name):
            return FILLS.index(name) % 2

        def fill_count(name):
            return FILLS.index(name) // 2 + 1

        def copied_count(name):
            return sum(fill_bank(k) == fill_bank(name) for k in COPIED[:COPIED.index(name) + 1])

        def split_count(name):
            return SPLITS.index(name) + 1

        def cols(ap, n, at=0):
            return ap[:, at:at + C * n].rearrange("p (c n) -> p c n", n=n)

        def tokens(tiles):
            return slice(tiles[0] * P, (tiles[-1] + 1) * P)

        def er(w, j):
            return w[:, j, :, :].rearrange("p e r -> p (e r)")

        def x1T_bank(h, j):
            return [cbank[2 * h], cbank[2 * h + 1], wide[0], wide[1]][j]

        def y_bank(i):
            return [*wide, *wide, *wide, cbank[0], cbank[1]][i]

        WR_AT, B_AT, PP_AT = C * E, 2 * C * E, 2 * C * E + C

        block = ctx.enter_context(nc.Block())

        @block.sync
        def _(sp):
            sp.dma_start(c0B_sb[:, :], er_rows(c0B)).then_inc(ld["c0B"], 16)
            sp.dma_start(x_sb[:, 0:2, :], x_tok[:, 0:2, :]).then_inc(ld["x01"], 16)
            sp.dma_start(x_sb[:, 2:4, :], x_tok[:, 2:4, :]).then_inc(ld["x23"], 16)
            sp.dma_start(f0W_sb[:, :, :], f0W.rearrange("(k p) d -> p k d", p=P)).then_inc(ld["f0W"], 16)
            sp.dma_start(f0A_sb[:, :], er_rows(f0A)).then_inc(ld["f0A"], 16)
            sp.dma_start(c0A_sb[:, :, :, :].rearrange("p e j r -> p e (j r)"), four_rows(c0A)).then_inc(ld["c0A"], 16)
            sp.dma_start(c1Wr_sb[:, :], c1Wr).then_inc(ld["small"], 16)
            sp.dma_start(f0b_sb[:, :], f0b.rearrange("(c p) -> c p", p=P)).then_inc(ld["small"], 16)
            sp.dma_start(pp_sb[0:ER4, :], er_rows(f1A)).then_inc(ld["pp"], 16)
            sp.dma_start(pp_sb[ER4:NPP, :], f1Wr).then_inc(ld["pp"], 16)
            sp.dma_start(x_sb[:, HALF:TILES, :], x_tok[:, HALF:TILES, :]).then_inc(ld["xh1"], 16)
            sp.dma_start(f0B_sb[:, :, :, :].rearrange("p e j r -> p e (j r)"), four_rows(f0B)).then_inc(ld["f0B"], 16)
            sp.dma_start(c1A_sb[:, :], er_rows(c1A)).then_inc(ld["c1A"], 16)
            sp.dma_start(c1W_sb[:, :, :], c1W.rearrange("(p j) d -> p j d", j=C)).then_inc(ld["c1W"], 16)
            sp.dma_start(c1B_sb[:, :, :, :].rearrange("p e j r -> p e (j r)"), four_rows(c1B)).then_inc(ld["c1B"], 16)
            sp.dma_start(f1B_sb[:, :, :, :].rearrange("p e j r -> p e (j r)"), four_rows(f1B)).then_inc(ld["f1B"], 16)
            for i in range(TILES):
                if i < TILES - 1:
                    sp.wait_ge(y_out, i + 1)
                else:
                    sp.wait_ge(last_y_out, 1)
                sp.dma_start(out_tok[:, i, :], out_sb[:, i, :]).then_inc(stored, 16)
            sp.wait_ge(stored, 16 * TILES)

        @block.gpsimd
        def _(pool):
            nc.gpsimd.memset(ident[:, :], 0.0).then_inc(pool_step, 1)
            pool.wait_ge(pool_step, 1)
            nc.gpsimd.affine_select(out=ident[:, :], in_=ident[:, :], compare_op=ALU.not_equal, fill=1.0, base=0,
                                    pattern=[[-1, P]], channel_multiplier=1).then_inc(consts_made, 1)
            nc.gpsimd.iota(part_i[:, :], pattern=[[0, 1]], base=0, channel_multiplier=1).then_inc(consts_made, 1)
            nc.gpsimd.iota(expert_i[:, :], pattern=[[1, E]], base=0, channel_multiplier=0).then_inc(consts_made, 1)
            nc.gpsimd.memset(lower8[:, :, :], 1.0).then_inc(pool_step, 1)
            pool.wait_ge(pool_step, 2)
            nc.gpsimd.affine_select(out=lower8[:, :, :], in_=lower8[:, :, :], compare_op=ALU.is_gt, fill=0.0, base=0,
                                    pattern=[[1, E], [-1, E]], channel_multiplier=0).then_inc(consts_made, 1)
            for e in range(E):
                nc.gpsimd.memset(terms8[:, :, e, E:E + 1], float(E - 1 - e))
            for e in range(E4):
                last = nc.gpsimd.memset(terms4[:, :, e, E4:E4 + 1], float(E4 - 1 - e))
            last.then_inc(consts_made, 1)

            def repack(k, src, dst):
                pool.wait_ge(ld[k], 16)
                nc.gpsimd.tensor_copy(dst[:, :, :, :], src[:, :, :, :].rearrange("p e j r -> p j e r")).then_inc(repacked, 1)

            def x_full(i):
                s = slice(i * P, (i + 1) * P)
                pool.wait_ge(lo_ready, split_count(f"x{i}"))
                nc.gpsimd.tensor_tensor(xT[:, :, s], xTs[0][:, :, s].bitcast(F32), xTs[1][:, :, s].bitcast(F32),
                                        ALU.add).then_inc(xT_ready, 1)

            repack("c0A", c0A_sb, c0A_er)
            for i in range(HALF):
                x_full(i)
            nc.gpsimd.memset(batch_of_token[:, :, :], 0.0).then_inc(pool_step, 1)
            pool.wait_ge(pool_step, 3)
            nc.gpsimd.affine_select(out=batch_of_token[:, :, :], in_=batch_of_token[:, :, :], compare_op=ALU.not_equal,
                                    fill=1.0, base=0, pattern=[[-1, NB], [0, S]],
                                    channel_multiplier=1).then_inc(consts_made, 1)
            repack("f0B", f0B_sb, f0B_er)
            repack("c1B", c1B_sb, c1B_er)
            repack("f1B", f1B_sb, f1B_er)
            for i in range(HALF, TILES):
                x_full(i)

        @block.scalar
        def _(act):
            act.dma_start(ids0_i[:, :], ids0.rearrange("(a b) -> a b", a=1).to_broadcast([P, NB])).then_inc(ld["ids"], 16)
            act.dma_start(ids1_i[:, :], ids1.rearrange("(b a) -> b a", a=1)).then_inc(ld["ids"], 16)
            act.dma_start(f0Wr_sb[:, :], f0Wr).then_inc(ld["router"], 16)

            exps_done = [0]

            def exps(e, tiles):
                exps_done[0] += 1
                act.wait_ge(shifted_ready, exps_done[0])
                n = len(tiles)
                nc.scalar.activation(expd[:, 0:n, 0:e], shifted[:, 0:n, 0:e], ACT.Exp).then_inc(exp_ready, 1)

            def take(name):
                act.wait_ge(filled[fill_bank(name)], fill_count(name))
                return tbank[fill_bank(name)]

            def free(name, ins):
                ins.then_inc(emptied[fill_bank(name)], 1)

            def x_tile(i):
                t = take(f"x{i}")
                nc.scalar.copy(xTs[0][:, :, i * P:(i + 1) * P], cols(t, P)).then_inc(hi_ready, 1)

            def H_half(h):
                s = tokens(HALVES[h])
                act.wait_ge(H_ready, h + 1)
                nc.scalar.copy(H[0][:, s], H_full[:, s]).then_inc(hi_ready, 1)

            def gated_T(name, tiles):
                t = take(name)
                nc.scalar.copy(gatedT[0][:, tokens(tiles)], t[:, 0:len(tiles) * P]).then_inc(hi_ready, 1)

            def mixed_T(name, tiles):
                t = take(name)
                nc.scalar.copy(mixedT[0:ER4, tokens(tiles)], t[0:ER4, 0:len(tiles) * P]).then_inc(hi_ready, 1)

            def gated_T1(name, tiles):
                t = take(name)
                free(name, nc.scalar.copy(gatedT1[:, tokens(tiles)], t[:, 0:len(tiles) * P]))

            def emit(i):
                act.wait_ge(y_done, i + 1)
                nc.scalar.copy(out_sb[:, i, :], y_bank(i)[:, :]).then_inc(y_out, 1)

            t = take("c0B")
            nc.scalar.copy(c0BT[0][:, :, :], cols(t, ER)).then_inc(hi_ready, 1)
            for i in range(HALF):
                x_tile(i)
            for j in (0, 2):
                t = take(f"fW{j}")
                free(f"fW{j}", nc.scalar.copy(f0T[:, j, 0:D], t[:, :]))
            H_half(0)
            t = take("small")
            nc.scalar.copy(f0T[:, :, D + ER:NM1], cols(t, E))
            nc.scalar.copy(bcol[:, :], t[:, B_AT:PP_AT])
            nc.scalar.copy(ppT[:, :, :], cols(t, NPP, PP_AT))
            free("small", nc.scalar.copy(Q[:, :, ER:ER + E], cols(t, E, WR_AT)))
            act.wait_ge(m1_wide_done, 1)
            nc.scalar.copy(M1[0][:, :], wide[1][:, :]).then_inc(hi_ready, 1)
            act.wait_ge(m1_narrow_done, 1)
            nc.scalar.copy(M1_narrow[:, :], cbank[3][:, 0:N0]).then_inc(narrow_ready, 1)
            x_tile(4)
            x_tile(5)
            exps(E, HALVES[0])
            x_tile(6)
            x_tile(7)
            t = take("f0B")
            free("f0B", nc.scalar.activation(o4(f0BT_full[:, :]), cols(t, P), ACT.Copy, scale=L0_SCALE))
            act.wait_ge(emptied[fill_bank("f0B")], copied_count("f0B"))
            nc.scalar.copy(f0BT[0][:, :], f0BT_full[:, :]).then_inc(hi_ready, 1)
            act.wait_ge(qp_done, 1)
            nc.scalar.copy(Q[:, :, ER + E:NQ], cols(wide[1], NPP)).then_inc(qp_ready, 1)
            gated_T("a0", HALVES[0])
            H_half(1)
            t = take("c1A")
            free("c1A", nc.scalar.copy(Q[:, :, 0:ER], cols(t, ER)))
            t = take("f1B")
            free("f1B", nc.scalar.activation(o4(f1BT_full[:, :]), cols(t[0:ER4, :], P), ACT.Copy, scale=FFN_SCALE))
            act.wait_ge(emptied[fill_bank("f1B")], copied_count("f1B"))
            nc.scalar.copy(f1BT_hi2[ER4:P, :], f1BT_full[:, :])
            nc.scalar.copy(f1BT_hi2[0:ER4, :], f1BT_full[:, :]).then_inc(hi_ready, 1)
            act.wait_ge(bp_done, 1)
            nc.scalar.activation(c1BP[:, :], wide[0][:, 0:NPP], ACT.Copy, scale=L1_SCALE).then_inc(bp_ready, 1)
            exps(E, HALVES[1])
            gated_T("a1", HALVES[1])
            exps(E, GROUPS[0])
            gated_T1("b0", GROUPS[0])
            exps(E4, GROUPS[0])
            exps(E, GROUPS[1])
            mixed_T("m0", GROUPS[0])
            gated_T1("b1", GROUPS[1])
            exps(E, GROUPS[2])
            gated_T1("b2", GROUPS[2])
            emit(0)
            emit(1)
            exps(E4, GROUPS[1])
            emit(2)
            emit(3)
            exps(E4, GROUPS[2])
            mixed_T("m1", GROUPS[1])
            mixed_T("m2", GROUPS[2])
            emit(4)
            emit(5)
            emit(6)

        @block.vector
        def _(dve):
            steps = [0]
            gates_done = [0]

            def count(ins):
                steps[0] += 1
                ins.then_inc(dve_step, 1)

            def step(ins):
                count(ins)
                dve.wait_ge(dve_step, steps[0])

            def take(name):
                dve.wait_ge(filled[fill_bank(name)], fill_count(name))
                return tbank[fill_bank(name)]

            def free(name, ins):
                ins.then_inc(emptied[fill_bank(name)], 1)

            def low(name, lo, full, hi):
                dve.wait_ge(hi_ready, split_count(name))
                return nc.vector.tensor_tensor(lo, full, hi.bitcast(F32), ALU.subtract).then_inc(lo_ready, 1)

            def low_T(name, lo, hi, n, rows=P):
                t = tbank[fill_bank(name)]
                low(name, lo, cols(t[0:rows, :], n) if len(lo.shape) == 3 else t[0:rows, 0:n], hi)

            def x_tile(i):
                s = slice(i * P, (i + 1) * P)
                low_T(f"x{i}", xTs[1][:, :, s], xTs[0][:, :, s], P)

            def H_half(h):
                s = tokens(HALVES[h])
                nb = NB // 2
                dve.wait_ge(h0_done, h + 1)
                m = mask0[:, h * nb:(h + 1) * nb].unsqueeze(2).to_broadcast([P, nb, S])
                nc.vector.tensor_tensor(H_full[:, s].rearrange("p (b s) -> p b s", s=S),
                                        wide[0][:, :].rearrange("p (b s) -> p b s", s=S), m, ALU.mult).then_inc(H_ready, 1)

            def H_low(h):
                s = tokens(HALVES[h])
                low(f"H{h}", H[1][:, s], H_full[:, s], H[0][:, s])

            def gate(tiles, e, w, log_at, h_at, terms):
                n = len(tiles)
                lg = logits[:, 0:n, 0:e]
                banks = [(k, cbank[tiles[k] // TPB][:, 0:TPB * w].rearrange("p (t n) -> p t n", n=w))
                         for k in range(0, n, TPB)]
                for k, b in banks:
                    last = nc.vector.tensor_copy(logits[:, k:k + TPB, 0:e], b[:, :, log_at:log_at + e])
                step(last)
                count(nc.vector.tensor_reduce(top[:, 0:n], lg, axis=AX_X, op=ALU.max))
                cm = cmp[:, 0:n, 0:e, 0:e]
                bf = before[:, 0:n, 0:e, 0:e]
                count(nc.vector.tensor_tensor(cm, lg.unsqueeze(2).to_broadcast([P, n, e, e]),
                                              lg.unsqueeze(3).to_broadcast([P, n, e, e]), ALU.is_ge))
                dve.wait_ge(dve_step, steps[0] - 1)
                nc.vector.tensor_tensor(shifted[:, 0:n, 0:e], lg, top[:, 0:n].unsqueeze(2).to_broadcast([P, n, e]),
                                        ALU.subtract).then_inc(shifted_ready, 1)
                dve.wait_ge(dve_step, steps[0])
                step(nc.vector.tensor_tensor(bf, cm, lower8[:, 0:e, 0:e].unsqueeze(1).to_broadcast([P, n, e, e]), ALU.mult))
                step(nc.vector.tensor_tensor(terms[:, 0:n, :, 0:e], bf, bf.rearrange("p t a b -> p t b a"), ALU.subtract))
                step(nc.vector.tensor_reduce(rank[:, 0:n, 0:e], terms[:, 0:n, :, :], axis=AX_X, op=ALU.add))
                gates_done[0] += 1
                dve.wait_ge(exp_ready, gates_done[0])
                step(nc.vector.scalar_tensor_tensor(out=picked[:, 0:n, 0:e], in0=rank[:, 0:n, 0:e], scalar=TOP_K,
                                                    in1=expd[:, 0:n, 0:e], op0=ALU.is_lt, op1=ALU.mult))
                step(nc.vector.reduce_sum(total[:, 0:n], picked[:, 0:n, 0:e], axis=AX_X))
                step(nc.vector.reciprocal(inv[:, 0:n], total[:, 0:n]))
                step(nc.vector.tensor_tensor(gates[:, 0:n, 0:e], picked[:, 0:n, 0:e],
                                             inv[:, 0:n].unsqueeze(2).to_broadcast([P, n, e]), ALU.mult))
                for k, b in banks:
                    last = nc.vector.tensor_tensor(
                        gated[:, tiles[k]:tiles[k] + TPB, 0:e * R].rearrange("p t (e r) -> p t e r", r=R),
                        b[:, :, h_at:h_at + e * R].rearrange("p t (e r) -> p t e r", r=R),
                        gates[:, k:k + TPB, 0:e].unsqueeze(3).to_broadcast([P, TPB, e, R]), ALU.mult)
                last.then_inc(gated_ready, 1)

            def x1T_half(h):
                s = tokens(HALVES[h])
                dve.wait_ge(xT_ready, HALF * (h + 1))
                for j in range(C):
                    dve.wait_ge(x1T_done, h * C + j + 1)
                    nc.vector.scalar_tensor_tensor(out=xT[:, j, s], in0=x1T_bank(h, j)[:, :], scalar=bcol[:, j:j + 1],
                                                   in1=xT[:, j, s], op0=ALU.add, op1=ALU.add).then_inc(x1T_ready, 1)

            def gated_low(name, tiles):
                s = tokens(tiles)
                low_T(name, gatedT[1][:, s], gatedT[0][:, s], len(tiles) * P)

            def mixed_low(name, tiles):
                s = tokens(tiles)
                low_T(name, mixedT[ER4:P, s], mixedT[0:ER4, s], len(tiles) * P, ER4)

            def gate0(tiles):
                gate(tiles, E, N0, ER, 0, terms8)

            def gate1(tiles):
                gate(tiles, E, NQ, ER, 0, terms8)

            def gate2(tiles):
                gate(tiles, E4, NQ, ER + E + ER4, ER + E, terms4)

            nc.vector.memset(lang_bias[:, :], 0.0).then_inc(setup_step, 1)
            dve.wait_ge(consts_made, 3)
            nc.vector.tensor_copy(part_f[:, :], part_i[:, :]).then_inc(setup_step, 1)
            nc.vector.tensor_copy(expert_f[:, :], expert_i[:, :]).then_inc(setup_step, 1)
            low_T("c0B", c0BT[1][:, :, :], c0BT[0][:, :, :], ER)
            for i in range(HALF):
                x_tile(i)
            dve.wait_ge(ld["ids"], 32)
            nc.vector.tensor_copy(ids0_f[:, :], ids0_i[:, :]).then_inc(setup_step, 1)
            nc.vector.tensor_copy(ids1_f[:, :], ids1_i[:, :]).then_inc(setup_step, 1)
            dve.wait_ge(setup_step, 5)
            nc.vector.tensor_scalar(mask0[:, :], ids0_f[:, :], -float(R), part_f[:, 0:1], ALU.mult,
                                    ALU.add).then_inc(setup_step, 1)
            nc.vector.tensor_scalar(lang_bias[0:NB, :], expert_f[0:NB, :], ids1_f[:, 0:1], LANG_BIAS, ALU.is_equal,
                                    ALU.mult).then_inc(lang_ready, 1)
            dve.wait_ge(setup_step, 6)
            nc.vector.tensor_single_scalar(below[:, :], mask0[:, :], float(R) - 0.5, op=ALU.is_lt).then_inc(setup_step, 1)
            dve.wait_ge(setup_step, 7)
            nc.vector.scalar_tensor_tensor(out=mask0[:, :], in0=mask0[:, :], scalar=-0.5, in1=below[:, :], op0=ALU.is_gt,
                                           op1=ALU.mult).then_inc(setup_step, 1)
            dve.wait_ge(setup_step, 8)
            H_half(0)
            for j in (1, 3):
                t = take(f"fW{j}")
                free(f"fW{j}", nc.vector.tensor_copy(f0T[:, j, 0:D], t[:, :]))
            H_low(0)
            t = take("f0A")
            free("f0A", nc.vector.tensor_copy(f0T[:, :, D:D + ER], cols(t, ER)))
            low("M1", M1[1][:, :], wide[1][:, :], M1[0][:, :])
            x_tile(4)
            x_tile(5)
            dve.wait_ge(consts_made, 5)
            dve.wait_ge(log0_done, 1)
            gate0(HALVES[0])
            x_tile(6)
            x_tile(7)
            low("f0B", f0BT[1][:, :], f0BT_full[:, :], f0BT[0][:, :])
            gated_low("a0", HALVES[0])
            H_half(1)
            H_low(1)
            low("f1B", f1BT_lo[:, :], f1BT_full[:, :], f1BT_hi2[0:ER4, :])
            dve.wait_ge(log0_done, 2)
            gate0(HALVES[1])
            x1T_half(0)
            gated_low("a1", HALVES[1])
            dve.wait_ge(log1_done, 1)
            gate1(GROUPS[0])
            x1T_half(1)
            dve.wait_ge(mid_done, 1)
            gate2(GROUPS[0])
            dve.wait_ge(log1_done, 2)
            gate1(GROUPS[1])
            dve.wait_ge(log1_done, 3)
            gate1(GROUPS[2])
            mixed_low("m0", GROUPS[0])
            dve.wait_ge(mid_done, 2)
            gate2(GROUPS[1])
            dve.wait_ge(mid_done, 3)
            gate2(GROUPS[2])
            mixed_low("m1", GROUPS[1])
            mixed_low("m2", GROUPS[2])
            dve.wait_ge(y_done, TILES)
            nc.vector.tensor_copy(out_sb[:, TILES - 1, :], y_bank(TILES - 1)[:, :]).then_inc(last_y_out, 1)

        @block.tensor
        def _(pe):
            def fill(name):
                n = FILLS.index(name)
                if n >= 2:
                    before = FILLS[n - 2]
                    if before in COPIED:
                        pe.wait_ge(emptied[fill_bank(before)], copied_count(before))
                    else:
                        pe.wait_ge(lo_ready, split_count(before))
                return tbank[fill_bank(name)]

            def done(name, ins):
                ins.then_inc(filled[fill_bank(name)], 1)

            def transposes(dst, n, src):
                for c in range(n):
                    s = src(c)
                    k, m = s.shape
                    last = nc.tensor.transpose(dst[0:m, c * k:(c + 1) * k], s, ident[0:k, 0:k])
                return last

            def split_matmul(dst, a, b, start, stop, skip=False):
                nc.tensor.matmul(dst, a[0], b[1], start=start, stop=False, skip_group_check=skip)
                nc.tensor.matmul(dst, a[0], b[0], start=False, stop=False, skip_group_check=skip)
                return nc.tensor.matmul(dst, a[1], b[0], start=False, stop=stop, skip_group_check=skip)

            def part(p, *idx):
                return p[0][idx], p[1][idx]

            def x_tile(i):
                n = f"x{i}"
                done(n, transposes(fill(n), C, lambda c: x_sb[:, i, c * P:(c + 1) * P]))

            def h0(h, tiles):
                pe.wait_ge(lo_ready, split_count(f"x{tiles[-1]}"))
                at = (tiles[0] - HALVES[h][0]) * P
                for c in range(C):
                    last = split_matmul(wide[0][:, at:at + len(tiles) * P], part(c0BT, slice(None), c),
                                        part(xTs, slice(None), c, tokens(tiles)), c == 0, c == C - 1, True)
                if tiles[-1] == HALVES[h][-1]:
                    last.then_inc(h0_done, 1)

            def warm(n):
                for _ in range(n):
                    nc.tensor.transpose(wide[1][:, 0:P], ident[:, :], ident[:, :])

            def log0(h):
                pe.wait_ge(H_ready, h + 1)
                for i in HALVES[h]:
                    o = (i % TPB) * N0
                    last = nc.tensor.matmul(cbank[i // TPB][:, o:o + N0], H_full[:, i * P:(i + 1) * P], M1_narrow[:, :],
                                            start=True, stop=True, skip_group_check=True)
                last.then_inc(log0_done, 1)

            def gated_T(name, n, tiles, rows=ER):
                pe.wait_ge(gated_ready, n)
                done(name, transposes(fill(name), len(tiles), lambda k: gated[:, tiles[k], 0:rows]))

            def x1T(h, chunks):
                s = tokens(HALVES[h])
                pe.wait_ge(lo_ready, split_count(f"a{h}"))
                for j in chunks:
                    b = x1T_bank(h, j)[:, :]
                    w = slice(j * P, (j + 1) * P)
                    split_matmul(b, part(M1, slice(None), w), part(H, slice(None), s), True, False)
                    split_matmul(b, part(f0BT, slice(None), w), part(gatedT, slice(None), s), False, True).then_inc(x1T_done, 1)

            def log1_part(tiles, chunks):
                for c in chunks:
                    pe.wait_ge(x1T_ready, tiles[0] // HALF * C + max(c + 1, 2 if len(tiles) > TPB or tiles[0] % HALF else 1))
                    for i in tiles:
                        o = (i % TPB) * NQ
                        nc.tensor.matmul(cbank[i // TPB][:, o:o + NQ], xT[:, c, i * P:(i + 1) * P], Q[:, c, :],
                                         start=(c == 0 and i % TPB == 0), stop=False, skip_group_check=True)

            def log1_bias(tiles):
                for i in tiles:
                    o = (i % TPB) * NQ + ER
                    last = nc.tensor.matmul(cbank[i // TPB][:, o:o + E],
                                            batch_of_token[:, i * (P // S):(i + 1) * (P // S), :].rearrange("p b s -> p (b s)"),
                                            lang_bias[:, :], start=False, stop=True, skip_group_check=True)
                last.then_inc(log1_done, 1)

            def mid(g):
                pe.wait_ge(emptied[fill_bank(f"b{g}")], copied_count(f"b{g}"))
                for i in GROUPS[g]:
                    o = (i % TPB) * NQ + ER + E
                    last = nc.tensor.matmul(cbank[i // TPB][:, o:o + NPP], gatedT1[:, i * P:(i + 1) * P], c1BP[:, :],
                                            start=False, stop=True, skip_group_check=True)
                last.then_inc(mid_done, 1)

            def y_back(tiles):
                for i in tiles:
                    if 2 <= i < 6:
                        pe.wait_ge(y_out, i - 1)
                    for c in range(C):
                        nc.tensor.matmul(y_bank(i)[:, c * P:(c + 1) * P], xT[:, c, i * P:(i + 1) * P], ident[:, :],
                                         is_transpose=True, start=(c == 0), stop=False, skip_group_check=True)

            def y(g, tiles):
                pe.wait_ge(lo_ready, split_count(f"m{g}"))
                for i in tiles:
                    b = y_bank(i)
                    s = slice(i * P, (i + 1) * P)
                    nc.tensor.matmul(b[:, :], mixedT[:, s], f1BT_hi2[:, :], start=False, stop=False, skip_group_check=True)
                    nc.tensor.matmul(b[:, :], mixedT[0:ER4, s], f1BT_lo[:, :], start=False, stop=True,
                                     skip_group_check=True).then_inc(y_done, 1)

            pe.wait_ge(consts_made, 1)
            warm(WARM[0])
            pe.wait_ge(ld["c0B"], 16)
            done("c0B", transposes(fill("c0B"), C, lambda c: c0B_sb[:, c * P:(c + 1) * P]))
            for i in range(HALF):
                if i % 2 == 0:
                    warm(WARM[1 + i // 2])
                    pe.wait_ge(ld[f"x{i}{i + 1}"], 16)
                x_tile(i)
            h0(0, range(0, TPB))
            h0(0, range(TPB, HALF))
            pe.wait_ge(ld["f0W"], 16)
            for j in range(C):
                n = f"fW{j}"
                done(n, transposes(fill(n), C, lambda k: o4(f0W_sb[:, k, :])[:, j, :]))
            pe.wait_ge(ld["f0A"], 16)
            done("f0A", transposes(fill("f0A"), C, lambda j: o4(f0A_sb[:, :])[:, j, :]))
            pe.wait_ge(ld["router"], 16)
            pe.wait_ge(ld["small"], 32)
            pe.wait_ge(ld["pp"], 32)
            b = fill("small")
            transposes(b, C, lambda j: o4(f0Wr_sb[:, :])[:, j, :])
            transposes(b[:, WR_AT:B_AT], C, lambda c: c1Wr_sb[:, c * P:(c + 1) * P])
            nc.tensor.transpose(b[:, B_AT:PP_AT], f0b_sb[:, :], ident[0:C, 0:C])
            done("small", transposes(b[:, PP_AT:PP_AT + C * NPP], C, lambda j: o4(pp_sb[:, :])[:, j, :]))
            pe.wait_ge(repacked, 1)
            for n in ("fW2", "fW3"):
                pe.wait_ge(emptied[fill_bank(n)], copied_count(n))
            for j in range(C):
                last = nc.tensor.matmul(wide[1][:, :], er(c0A_er, j), f0T[:, j, 0:D], start=(j == 0), stop=(j == C - 1))
            last.then_inc(m1_wide_done, 1)
            for n in ("f0A", "small"):
                pe.wait_ge(emptied[fill_bank(n)], copied_count(n))
            for j in range(C):
                last = nc.tensor.matmul(cbank[3][:, 0:N0], er(c0A_er, j), f0T[:, j, D:NM1], start=(j == 0), stop=(j == C - 1))
            last.then_inc(m1_narrow_done, 1)
            pe.wait_ge(ld["xh1"], 16)
            x_tile(4)
            x_tile(5)
            pe.wait_ge(narrow_ready, 1)
            log0(0)
            x_tile(6)
            x_tile(7)
            pe.wait_ge(ld["c1W"], 16)
            pe.wait_ge(lo_ready, split_count("M1"))
            for c in range(C):
                for j in range(C):
                    last = nc.tensor.matmul(wide[1][:, c * NPP:(c + 1) * NPP], c1W_sb[:, j, c * P:(c + 1) * P], ppT[:, j, :],
                                            start=(j == 0), stop=(j == C - 1), skip_group_check=True)
            last.then_inc(qp_done, 1)
            pe.wait_ge(repacked, 2)
            done("f0B", transposes(fill("f0B"), C, lambda j: er(f0B_er, j)))
            gated_T("a0", 1, HALVES[0])
            h0(1, HALVES[1])
            pe.wait_ge(ld["c1A"], 16)
            done("c1A", transposes(fill("c1A"), C, lambda c: c1A_sb[:, c * P:(c + 1) * P]))
            pe.wait_ge(repacked, 4)
            done("f1B", transposes(fill("f1B"), C, lambda j: er(f1B_er, j)))
            log0(1)
            for j in range(C):
                last = nc.tensor.matmul(wide[0][:, 0:NPP], er(c1B_er, j), ppT[:, j, :], start=(j == 0), stop=(j == C - 1))
            last.then_inc(bp_done, 1)
            x1T(0, [0, 1])
            pe.wait_ge(qp_ready, 1)
            pe.wait_ge(bp_ready, 1)
            x1T(0, [2, 3])
            gated_T("a1", 2, HALVES[1])
            pe.wait_ge(consts_made, 6)
            pe.wait_ge(lang_ready, 1)
            log1_part(GROUPS[0], range(C))
            log1_bias(GROUPS[0])
            x1T(1, [0, 1, 2])
            gated_T("b0", 3, GROUPS[0])
            x1T(1, [3])
            mid(0)
            log1_part(GROUPS[1], range(C))
            log1_bias(GROUPS[1])
            log1_part(GROUPS[2], [0, 1, 2])
            gated_T("m0", 4, GROUPS[0], ER4)
            log1_part(GROUPS[2], [3])
            log1_bias(GROUPS[2])
            gated_T("b1", 5, GROUPS[1])
            y_back([0, 1])
            mid(1)
            gated_T("b2", 6, GROUPS[2])
            y(0, [0, 1])
            mid(2)
            y_back([6, 7])
            y_back([2, 3])
            y(0, [2, 3])
            gated_T("m1", 7, GROUPS[1], ER4)
            y_back([4, 5])
            gated_T("m2", 8, GROUPS[2], ER4)
            y(1, GROUPS[1])
            y(2, GROUPS[2])


_INS = ['x', 'itok_B_3_7', 'itok_B_0_7', 'L0_cond_A', 'L0_cond_B', 'L0_ffn_W_base', 'L0_ffn_b_base', 'L0_ffn_W_router',
        'L0_ffn_A', 'L0_ffn_B', 'L1_cond_W', 'L1_cond_Wr', 'L1_cond_A', 'L1_cond_B', 'L1_ffn_A', 'L1_ffn_B', 'L1_ffn_Wr']
_OUTS = [((32, 32, 512), 'float32')]


def kernel(**inputs):
    import numpy as _np
    import concourse.bacc as _bacc
    from concourse import mybir as _mybir
    from concourse.bass_utils import run_bass_kernel_spmd as _run

    nc = _bacc.Bacc("TRN2", target_bir_lowering=False, num_devices=1)
    arrays, args = {}, []
    for name in _INS:
        a = _np.ascontiguousarray(inputs[name])
        arrays[f"in_{name}_dram"] = a
        args.append(nc.dram_tensor(f"in_{name}_dram", a.shape, _mybir.dt.from_np(a.dtype), kind="ExternalInput").ap())
    for i, (shape, dtype) in enumerate(_OUTS):
        dt = _mybir.dt.from_np(_np.dtype(dtype))
        args.append(nc.dram_tensor(f"out_{i}_dram", shape, dt, kind="ExternalOutput").ap())
    adaln_ffn_two_layers(nc, *args)
    r = _run(nc, [arrays], core_ids=[0])
    got = tuple(r.results[0][f"out_{i}_dram"] for i in range(len(_OUTS)))
    return got[0]
```

```python
from contextlib import ExitStack

import concourse.bass as bass
from concourse import mybir

P = 128
F32 = mybir.dt.float32
I32 = mybir.dt.int32
F32R = mybir.dt.float32r
BF16 = mybir.dt.bfloat16
ALU = mybir.AluOpType
ACT = mybir.ActivationFunctionType
AX_X = mybir.AxisListType.X

L0_SCALE = 32.0 / 16.0
L1_SCALE = 32.0 / 16.0
FFN_SCALE = 16.0 / 16.0 ** 0.5
LANG_BIAS = 5.0
TOP_K = 2.0
LEAST = 2.0 ** -126


def adaln_ffn_two_layers(nc, x, ids0, ids1, c0A, c0B, f0W, f0b, f0Wr, f0A, f0B, c1W, c1Wr, c1A, c1B, f1A, f1B, f1Wr, out):
    NB, S, D = x.shape
    N = NB * S
    TILES = N // P
    HALF = TILES // 2
    C = D // P
    E, R = c0B.shape[0], c0B.shape[1]
    ER = E * R
    E4 = f1A.shape[0]
    ER4 = E4 * R
    NPP = ER4 + E4
    N0 = ER + E
    NQ = ER + E + NPP
    TPB = 2
    GROUPS = [range(0, 4), range(4, 6), range(6, 8)]
    HALVES = [range(0, HALF), range(HALF, TILES)]
    assert ER == P and 2 * ER4 == P and D == 4 * P and TPB * NQ <= 512 and TILES == 8

    FILLS = [["c0B", "x3", "small", "x5", "a0", "f1B", "b0", "b1", "b2", "m2"],
             ["x0", "f0A", "x4", "x7", "c1A", "a1", "m0", "m1"],
             ["x1", "fW0"], ["x2", "fW1"], ["fW2", "x6"], ["fW3", "f0B"]]
    COPIED = ["f0A", "small", "f0B", "c1A", "f1B", "b0", "b1", "b2"]
    SPLITS = ["c0B", "x0", "x1", "x2", "x3", "fW0", "c0A", "fW1", "fW2", "fW3", "H0", "M1", "x4", "x5", "x6", "x7",
              "f0B", "a0", "H1", "f1B", "a1", "m0", "m1", "m2"]

    with ExitStack() as ctx:
        def sb(name, shape, dt=F32):
            return ctx.enter_context(nc.sbuf_tensor(name, shape, dt))

        def bank(name):
            return ctx.enter_context(nc.psum_tensor(name, [P, 512], F32))

        def sem(name):
            return ctx.enter_context(nc.semaphore(name))

        def pair(name, shape):
            return sb(name + "_hi", shape, F32R), sb(name + "_lo", shape, F32R)

        x_sb = sb("x_sb", [P, TILES, D])
        c0B_sb = sb("c0B_sb", [P, D])
        c0A_sb = sb("c0A_sb", [P, E, C, R])
        f0W_sb = sb("f0W_sb", [P, C, D])
        f0A_sb = sb("f0A_sb", [P, D])
        f0Wr_sb = sb("f0Wr_sb", [E, D])
        f0b_sb = sb("f0b_sb", [C, P])
        f0B_sb = sb("f0B_sb", [P, E, C, R])
        c1W_sb = sb("c1W_sb", [P, C, D])
        c1Wr_sb = sb("c1Wr_sb", [E, D])
        c1A_sb = sb("c1A_sb", [P, D])
        c1B_sb = sb("c1B_sb", [P, E, C, R])
        pp_sb = sb("pp_sb", [NPP, D])
        f1B_sb = sb("f1B_sb", [P, E4, C, R])
        ids0_i = sb("ids0_i", [P, NB], I32)
        ids1_i = sb("ids1_i", [NB, 1], I32)

        c0A_er = sb("c0A_er", [P, C, E, R])
        f0B_er = sb("f0B_er", [P, C, E, R])
        c1B_er = sb("c1B_er", [P, C, E, R])
        f1B_er = sb("f1B_er", [P, C, E4, R])

        ident = sb("ident", [P, P])
        batch_of_token = sb("batch_of_token", [P, NB, S], BF16)
        part_i = sb("part_i", [P, 1], I32)
        part_f = sb("part_f", [P, 1])
        expert_i = sb("expert_i", [P, E], I32)
        expert_f = sb("expert_f", [P, E])
        at_least = sb("at_least", [P, E, E])

        ids0_f = sb("ids0_f", [P, NB])
        ids1_f = sb("ids1_f", [NB, 1])
        below = sb("below", [P, NB])
        mask0 = sb("mask0", [P, NB])
        lang_bias = sb("lang_bias", [P, E], BF16)
        c0BT = pair("c0BT", [P, C, ER])
        c0A_split = pair("c0A", [P, C, E, R])
        f0WT = pair("f0WT", [P, C, D])
        f0T_narrow = sb("f0T_narrow", [P, C, N0])
        M1 = pair("M1", [P, D])
        M1_narrow = sb("M1_narrow", [P, N0])
        f0BT = pair("f0BT", [P, D])
        bcol = sb("bcol", [P, C])
        ppT = sb("ppT", [P, C, NPP])
        Q = sb("Q", [P, C, NQ])
        c1BP = sb("c1BP", [P, NPP])
        f1BT_hi2 = sb("f1BT_hi2", [P, D], F32R)
        f1BT_lo = sb("f1BT_lo", [ER4, D], F32R)
        BT_full = sb("BT_full", [P, D])

        xT = sb("xT", [P, C, N])
        xTs = pair("xTs", [P, C, N])
        H_full = sb("H_full", [P, N])
        H = pair("H", [P, N])
        logits = sb("logits", [P, HALF, E])
        top = sb("top", [P, HALF])
        shifted = sb("shifted", [P, HALF, E])
        expd = sb("expd", [P, HALF, E])
        ahead = sb("ahead", [P, HALF, E, E])
        before = sb("before", [P, HALF, E, E], BF16)
        rank = sb("rank", [P, HALF, E])
        picked = sb("picked", [P, HALF, E])
        total = sb("total", [P, HALF])
        inv = sb("inv", [P, HALF])
        gated = sb("gated", [P, TILES, ER])
        gatedT = pair("gatedT", [P, N])
        gatedT1 = sb("gatedT1", [P, N])
        mixedT = sb("mixedT", [P, N], F32R)
        out_sb = sb("out_sb", [P, TILES, D])

        wide = [bank("w0"), bank("w1")]
        cbank = [bank(f"c{i}") for i in range(TILES // TPB)]
        tbank = [bank("t0"), bank("t1"), *cbank]

        ld = {k: sem("ld_" + k) for k in ("c0B", "x01", "x23", "xh1", "c0A", "f0W", "f0A", "small", "router", "ids",
                                          "f0B", "c1W", "c1A", "c1B", "f1B", "pp")}
        filled = [sem(f"filled{k}") for k in range(len(FILLS))]
        emptied = [sem(f"emptied{k}") for k in range(len(FILLS))]
        hi_ready = sem("hi_ready")
        lo_ready = sem("lo_ready")
        consts_made = sem("consts_made")
        repacked = sem("repacked")
        pool_step = sem("pool_step")
        setup_step = sem("setup_step")
        lang_ready = sem("lang_ready")
        h0_done = sem("h0_done")
        H_ready = sem("H_ready")
        m1_wide_done = sem("m1_wide_done")
        m1_narrow_done = sem("m1_narrow_done")
        log0_done = sem("log0_done")
        narrow_ready = sem("narrow_ready")
        qp_done = sem("qp_done")
        qp_ready = sem("qp_ready")
        bp_done = sem("bp_done")
        bp_ready = sem("bp_ready")
        xT_ready = sem("xT_ready")
        shifted_ready = sem("shifted_ready")
        exp_ready = sem("exp_ready")
        gated_ready = sem("gated_ready")
        x1T_done = sem("x1T_done")
        x1T_ready = sem("x1T_ready")
        log1_done = sem("log1_done")
        mid_done = sem("mid_done")
        y_done = sem("y_done")
        y_out = sem("y_out")
        tile6_out = sem("tile6_out")
        stored = sem("stored")
        dve_step = sem("dve_step")

        x_tok = x.rearrange("b s d -> (b s) d").rearrange("(i p) d -> p i d", p=P)
        out_tok = out.rearrange("b s d -> (b s) d").rearrange("(i p) d -> p i d", p=P)

        def er_rows(w):
            return w.rearrange("e r d -> (e r) d")

        def four_rows(w):
            return w.rearrange("e (p j) r -> p e (j r)", j=C)

        def o4(ap):
            return ap.rearrange("q (p j) -> q j p", j=C)

        def fill_bank(name):
            return next(k for k, fills in enumerate(FILLS) if name in fills)

        def fill_count(name):
            return FILLS[fill_bank(name)].index(name) + 1

        def copied_count(name):
            return sum(k in COPIED for k in FILLS[fill_bank(name)][:fill_count(name)])

        def split_count(name):
            return SPLITS.index(name) + 1

        def cols(ap, n, at=0):
            return ap[:, at:at + C * n].rearrange("p (c n) -> p c n", n=n)

        def tokens(tiles):
            return slice(tiles[0] * P, (tiles[-1] + 1) * P)

        def er(w, j):
            return w[:, j, :, :].rearrange("p e r -> p (e r)")

        def x1T_bank(h, j):
            return [cbank[2 * h], cbank[2 * h + 1], wide[0], wide[1]][j]

        def y_bank(i):
            return [*wide, *cbank[0:3], *wide, cbank[0]][i]

        WR_AT, B_AT, PP_AT = C * E, 2 * C * E, 2 * C * E + C

        block = ctx.enter_context(nc.Block())

        @block.sync
        def _(sp):
            sp.dma_start(c0B_sb[:, :], er_rows(c0B)).then_inc(ld["c0B"], 16)
            sp.dma_start(x_sb[:, 0:2, :], x_tok[:, 0:2, :]).then_inc(ld["x01"], 16)
            sp.dma_start(x_sb[:, 2:4, :], x_tok[:, 2:4, :]).then_inc(ld["x23"], 16)
            sp.dma_start(f0W_sb[:, :, :], f0W.rearrange("(k p) d -> p k d", p=P)).then_inc(ld["f0W"], 16)
            sp.dma_start(c0A_sb[:, :, :, :].rearrange("p e j r -> p e (j r)"), four_rows(c0A)).then_inc(ld["c0A"], 16)
            sp.dma_start(f0A_sb[:, :], er_rows(f0A)).then_inc(ld["f0A"], 16)
            sp.dma_start(c1Wr_sb[:, :], c1Wr).then_inc(ld["small"], 16)
            sp.dma_start(f0b_sb[:, :], f0b.rearrange("(c p) -> c p", p=P)).then_inc(ld["small"], 16)
            sp.dma_start(pp_sb[0:ER4, :], er_rows(f1A)).then_inc(ld["pp"], 16)
            sp.dma_start(pp_sb[ER4:NPP, :], f1Wr).then_inc(ld["pp"], 16)
            sp.dma_start(x_sb[:, HALF:TILES, :], x_tok[:, HALF:TILES, :]).then_inc(ld["xh1"], 16)
            sp.dma_start(c1W_sb[:, :, :], c1W.rearrange("(p j) d -> p j d", j=C)).then_inc(ld["c1W"], 16)
            sp.dma_start(f0B_sb[:, :, :, :].rearrange("p e j r -> p e (j r)"), four_rows(f0B)).then_inc(ld["f0B"], 16)
            sp.dma_start(c1A_sb[:, :], er_rows(c1A)).then_inc(ld["c1A"], 16)
            sp.dma_start(c1B_sb[:, :, :, :].rearrange("p e j r -> p e (j r)"), four_rows(c1B)).then_inc(ld["c1B"], 16)
            sp.dma_start(f1B_sb[:, :, :, :].rearrange("p e j r -> p e (j r)"), four_rows(f1B)).then_inc(ld["f1B"], 16)
            for i in range(TILES):
                if i == TILES - 2:
                    sp.wait_ge(tile6_out, 1)
                else:
                    sp.wait_ge(y_out, min(i + 1, TILES - 1))
                sp.dma_start(out_tok[:, i, :], out_sb[:, i, :]).then_inc(stored, 16)
            sp.wait_ge(stored, 16 * TILES)

        @block.gpsimd
        def _(pool):
            nc.gpsimd.memset(ident[:, :], 0.0).then_inc(pool_step, 1)
            pool.wait_ge(pool_step, 1)
            nc.gpsimd.affine_select(out=ident[:, :], in_=ident[:, :], compare_op=ALU.not_equal, fill=1.0, base=0,
                                    pattern=[[-1, P]], channel_multiplier=1).then_inc(consts_made, 1)
            nc.gpsimd.iota(part_i[:, :], pattern=[[0, 1]], base=0, channel_multiplier=1).then_inc(consts_made, 1)
            nc.gpsimd.iota(expert_i[:, :], pattern=[[1, E]], base=0, channel_multiplier=0).then_inc(consts_made, 1)
            nc.gpsimd.memset(at_least[:, :, :], 0.0).then_inc(pool_step, 1)
            pool.wait_ge(pool_step, 2)
            nc.gpsimd.affine_select(out=at_least[:, :, :], in_=at_least[:, :, :], compare_op=ALU.is_gt, fill=LEAST,
                                    base=0, pattern=[[1, E], [-1, E]], channel_multiplier=0).then_inc(consts_made, 1)

            def repack(k, src, dst):
                pool.wait_ge(ld[k], 16)
                nc.gpsimd.tensor_copy(dst[:, :, :, :], src[:, :, :, :].rearrange("p e j r -> p j e r")).then_inc(repacked, 1)

            def x_full(i):
                s = slice(i * P, (i + 1) * P)
                pool.wait_ge(lo_ready, split_count(f"x{i}"))
                nc.gpsimd.tensor_tensor(xT[:, :, s], xTs[0][:, :, s].bitcast(F32), xTs[1][:, :, s].bitcast(F32),
                                        ALU.add).then_inc(xT_ready, 1)

            repack("c0A", c0A_sb, c0A_er)
            for i in range(HALF):
                x_full(i)
            nc.gpsimd.memset(batch_of_token[:, :, :], 0.0).then_inc(pool_step, 1)
            pool.wait_ge(pool_step, 3)
            nc.gpsimd.affine_select(out=batch_of_token[:, :, :], in_=batch_of_token[:, :, :], compare_op=ALU.not_equal,
                                    fill=1.0, base=0, pattern=[[-1, NB], [0, S]],
                                    channel_multiplier=1).then_inc(consts_made, 1)
            repack("f0B", f0B_sb, f0B_er)
            repack("c1B", c1B_sb, c1B_er)
            repack("f1B", f1B_sb, f1B_er)
            for i in range(HALF, TILES):
                x_full(i)

        @block.scalar
        def _(act):
            act.dma_start(ids0_i[:, :], ids0.rearrange("(a b) -> a b", a=1).to_broadcast([P, NB])).then_inc(ld["ids"], 16)
            act.dma_start(ids1_i[:, :], ids1.rearrange("(b a) -> b a", a=1)).then_inc(ld["ids"], 16)
            act.dma_start(f0Wr_sb[:, :], f0Wr).then_inc(ld["router"], 16)

            exps_done = [0]

            def exps(e, tiles):
                exps_done[0] += 1
                act.wait_ge(shifted_ready, exps_done[0])
                n = len(tiles)
                nc.scalar.activation(expd[:, 0:n, 0:e], shifted[:, 0:n, 0:e],
                                     ACT.Exp).then_inc(exp_ready, 1)

            def take(name):
                act.wait_ge(filled[fill_bank(name)], fill_count(name))
                return tbank[fill_bank(name)]

            def free(name, ins):
                ins.then_inc(emptied[fill_bank(name)], 1)

            def x_tile(i):
                t = take(f"x{i}")
                nc.scalar.copy(xTs[0][:, :, i * P:(i + 1) * P], cols(t, P)).then_inc(hi_ready, 1)

            def f0W_chunk(j):
                t = take(f"fW{j}")
                nc.scalar.copy(f0WT[0][:, j, :], t[:, :]).then_inc(hi_ready, 1)

            def H_half(h):
                s = tokens(HALVES[h])
                act.wait_ge(H_ready, h + 1)
                nc.scalar.copy(H[0][:, s], H_full[:, s]).then_inc(hi_ready, 1)

            def gated_T(name, tiles):
                t = take(name)
                nc.scalar.copy(gatedT[0][:, tokens(tiles)], t[:, 0:len(tiles) * P]).then_inc(hi_ready, 1)

            def mixed_T(name, tiles):
                t = take(name)
                nc.scalar.copy(mixedT[0:ER4, tokens(tiles)], t[0:ER4, 0:len(tiles) * P]).then_inc(hi_ready, 1)

            def gated_T1(name, tiles):
                t = take(name)
                free(name, nc.scalar.copy(gatedT1[:, tokens(tiles)], t[:, 0:len(tiles) * P]))

            def emit(i):
                act.wait_ge(y_done, i + 1)
                nc.scalar.copy(out_sb[:, i, :], y_bank(i)[:, :]).then_inc(y_out, 1)

            t = take("c0B")
            nc.scalar.copy(c0BT[0][:, :, :], cols(t, ER)).then_inc(hi_ready, 1)
            for i in range(HALF):
                x_tile(i)
            f0W_chunk(0)
            act.wait_ge(ld["c0A"], 16)
            nc.scalar.copy(c0A_split[0][:, :, :, :], c0A_sb[:, :, :, :].rearrange("p e j r -> p j e r")).then_inc(hi_ready, 1)
            for j in range(1, C):
                f0W_chunk(j)
            H_half(0)
            t = take("f0A")
            free("f0A", nc.scalar.copy(f0T_narrow[:, :, 0:ER], cols(t, ER)))
            t = take("small")
            nc.scalar.copy(f0T_narrow[:, :, ER:N0], cols(t, E))
            nc.scalar.copy(bcol[:, :], t[:, B_AT:PP_AT])
            nc.scalar.copy(ppT[:, :, :], cols(t, NPP, PP_AT))
            free("small", nc.scalar.copy(Q[:, :, ER:ER + E], cols(t, E, WR_AT)))
            act.wait_ge(m1_wide_done, 1)
            nc.scalar.copy(M1[0][:, :], wide[1][:, :]).then_inc(hi_ready, 1)
            act.wait_ge(m1_narrow_done, 1)
            nc.scalar.copy(M1_narrow[:, :], cbank[3][:, 0:N0]).then_inc(narrow_ready, 1)
            x_tile(4)
            x_tile(5)
            exps(E, HALVES[0])
            x_tile(6)
            x_tile(7)
            t = take("f0B")
            free("f0B", nc.scalar.activation(o4(BT_full[:, :]), cols(t, P), ACT.Copy, scale=L0_SCALE))
            act.wait_ge(emptied[fill_bank("f0B")], copied_count("f0B"))
            nc.scalar.copy(f0BT[0][:, :], BT_full[:, :]).then_inc(hi_ready, 1)
            act.wait_ge(qp_done, 1)
            nc.scalar.copy(Q[:, :, ER + E:NQ], cols(wide[1], NPP)).then_inc(qp_ready, 1)
            gated_T("a0", HALVES[0])
            H_half(1)
            t = take("c1A")
            free("c1A", nc.scalar.copy(Q[:, :, 0:ER], cols(t, ER)))
            act.wait_ge(bp_done, 1)
            nc.scalar.activation(c1BP[:, :], wide[0][:, 0:NPP], ACT.Copy, scale=L1_SCALE).then_inc(bp_ready, 1)
            act.wait_ge(lo_ready, split_count("f0B"))
            t = take("f1B")
            free("f1B", nc.scalar.activation(o4(BT_full[0:ER4, :]), cols(t[0:ER4, :], P), ACT.Copy, scale=FFN_SCALE))
            act.wait_ge(emptied[fill_bank("f1B")], copied_count("f1B"))
            nc.scalar.copy(f1BT_hi2[ER4:P, :], BT_full[0:ER4, :])
            nc.scalar.copy(f1BT_hi2[0:ER4, :], BT_full[0:ER4, :]).then_inc(hi_ready, 1)
            exps(E, HALVES[1])
            gated_T("a1", HALVES[1])
            exps(E, GROUPS[0])
            gated_T1("b0", GROUPS[0])
            exps(E4, GROUPS[0])
            exps(E, GROUPS[1])
            mixed_T("m0", GROUPS[0])
            gated_T1("b1", GROUPS[1])
            exps(E, GROUPS[2])
            exps(E4, GROUPS[1])
            gated_T1("b2", GROUPS[2])
            for i in range(3):
                emit(i)
            exps(E4, GROUPS[2])
            emit(3)
            mixed_T("m1", GROUPS[1])
            mixed_T("m2", GROUPS[2])
            emit(4)
            emit(5)
            emit(7)

        @block.vector
        def _(dve):
            steps = [0]
            gates_done = [0]

            def count(ins):
                steps[0] += 1
                ins.then_inc(dve_step, 1)
                return steps[0]

            def low(name, lo, full, hi):
                dve.wait_ge(hi_ready, split_count(name))
                return nc.vector.tensor_tensor(lo, full, hi.bitcast(F32), ALU.subtract).then_inc(lo_ready, 1)

            def low_T(name, lo, hi, n, rows=P):
                t = tbank[fill_bank(name)]
                low(name, lo, cols(t[0:rows, :], n) if len(lo.shape) == 3 else t[0:rows, 0:n], hi)

            def x_tile(i):
                s = slice(i * P, (i + 1) * P)
                low_T(f"x{i}", xTs[1][:, :, s], xTs[0][:, :, s], P)

            def x_tiles(*tiles):
                for i in tiles:
                    yield
                    yield
                    x_tile(i)

            def f0W_low(j):
                low_T(f"fW{j}", f0WT[1][:, j, :], f0WT[0][:, j, :], D)

            def H_half(h):
                s = tokens(HALVES[h])
                nb = NB // 2
                dve.wait_ge(h0_done, h + 1)
                m = mask0[:, h * nb:(h + 1) * nb].unsqueeze(2).to_broadcast([P, nb, S])
                nc.vector.tensor_tensor(H_full[:, s].rearrange("p (b s) -> p b s", s=S),
                                        wide[0][:, :].rearrange("p (b s) -> p b s", s=S), m, ALU.mult).then_inc(H_ready, 1)

            def H_low(h):
                s = tokens(HALVES[h])
                low(f"H{h}", H[1][:, s], H_full[:, s], H[0][:, s])

            def in_turn(*jobs):
                jobs = list(jobs)
                while jobs:
                    jobs = [job for job in jobs if next(job, "over") != "over"]

            def gate(tiles, e, w, log_at, h_at):
                n = len(tiles)
                lg = logits[:, 0:n, 0:e]
                ah = ahead[:, 0:n, 0:e, 0:e]
                bf = before[:, 0:n, 0:e, 0:e]
                sh = shifted[:, 0:n, 0:e]
                ex = expd[:, 0:n, 0:e]
                pk = picked[:, 0:n, 0:e]
                tot = total[:, 0:n]
                banks = [(k, cbank[tiles[k] // TPB][:, 0:TPB * w].rearrange("p (t n) -> p t n", n=w))
                         for k in range(0, n, TPB)]
                for k, b in banks:
                    at = count(nc.vector.tensor_copy(lg[:, k:k + TPB, :], b[:, :, log_at:log_at + e]))
                yield
                dve.wait_ge(dve_step, at)
                topped = count(nc.vector.tensor_reduce(top[:, 0:n], lg, axis=AX_X, op=ALU.max))
                at = count(nc.vector.tensor_tensor(ah, lg.unsqueeze(2).to_broadcast([P, n, e, e]),
                                                   lg.unsqueeze(3).to_broadcast([P, n, e, e]), ALU.subtract))
                dve.wait_ge(dve_step, topped)
                nc.vector.tensor_tensor(sh, lg, top[:, 0:n].unsqueeze(2).to_broadcast([P, n, e]),
                                        ALU.subtract).then_inc(shifted_ready, 1)
                yield
                dve.wait_ge(dve_step, at)
                at = count(nc.vector.tensor_tensor(bf, ah, at_least[:, 0:e, 0:e].unsqueeze(1).to_broadcast([P, n, e, e]),
                                                   ALU.is_ge))
                yield
                dve.wait_ge(dve_step, at)
                at = count(nc.vector.tensor_reduce(rank[:, 0:n, 0:e], bf, axis=AX_X, op=ALU.add))
                yield
                gates_done[0] += 1
                dve.wait_ge(exp_ready, gates_done[0])
                dve.wait_ge(dve_step, at)
                at = count(nc.vector.scalar_tensor_tensor(out=pk, in0=rank[:, 0:n, 0:e], scalar=TOP_K, in1=ex,
                                                          op0=ALU.is_lt, op1=ALU.mult))
                yield
                dve.wait_ge(dve_step, at)
                at = count(nc.vector.reduce_sum(tot, pk, axis=AX_X))
                yield
                dve.wait_ge(dve_step, at)
                at = count(nc.vector.reciprocal(inv[:, 0:n], tot))
                yield
                dve.wait_ge(dve_step, at)
                for k in range(n):
                    b = banks[k // TPB][1]
                    last = nc.vector.scalar_tensor_tensor(
                        out=gated[:, tiles[k], 0:e * R].rearrange("p (e r) -> p e r", r=R),
                        in0=pk[:, k, :].unsqueeze(2).to_broadcast([P, e, R]), scalar=inv[:, k:k + 1],
                        in1=b[:, k % TPB, h_at:h_at + e * R].rearrange("p (e r) -> p e r", r=R),
                        op0=ALU.mult, op1=ALU.mult)
                last.then_inc(gated_ready, 1)

            def x1T_half(h):
                s = tokens(HALVES[h])
                dve.wait_ge(xT_ready, HALF * (h + 1))
                for j in range(C):
                    dve.wait_ge(x1T_done, h * C + j + 1)
                    nc.vector.scalar_tensor_tensor(out=xT[:, j, s], in0=x1T_bank(h, j)[:, :], scalar=bcol[:, j:j + 1],
                                                   in1=xT[:, j, s], op0=ALU.add, op1=ALU.add).then_inc(x1T_ready, 1)
                    yield

            def gated_low(name, tiles):
                s = tokens(tiles)
                low_T(name, gatedT[1][:, s], gatedT[0][:, s], len(tiles) * P)

            def mixed_low(name, tiles):
                s = tokens(tiles)
                low_T(name, mixedT[ER4:P, s], mixedT[0:ER4, s], len(tiles) * P, ER4)

            def gate0(h):
                dve.wait_ge(log0_done, h + 1)
                yield from gate(HALVES[h], E, N0, ER, 0)

            def gate1(g):
                dve.wait_ge(log1_done, g + 1)
                yield from gate(GROUPS[g], E, NQ, ER, 0)

            def gate2(g):
                dve.wait_ge(mid_done, g + 1)
                yield from gate(GROUPS[g], E4, NQ, ER + E + ER4, ER + E)

            nc.vector.memset(lang_bias[:, :], 0.0).then_inc(setup_step, 1)
            dve.wait_ge(consts_made, 3)
            nc.vector.tensor_copy(part_f[:, :], part_i[:, :]).then_inc(setup_step, 1)
            nc.vector.tensor_copy(expert_f[:, :], expert_i[:, :]).then_inc(setup_step, 1)
            low_T("c0B", c0BT[1][:, :, :], c0BT[0][:, :, :], ER)
            for i in range(HALF):
                x_tile(i)
            dve.wait_ge(ld["ids"], 32)
            nc.vector.tensor_copy(ids0_f[:, :], ids0_i[:, :]).then_inc(setup_step, 1)
            nc.vector.tensor_copy(ids1_f[:, :], ids1_i[:, :]).then_inc(setup_step, 1)
            dve.wait_ge(setup_step, 5)
            nc.vector.tensor_scalar(mask0[:, :], ids0_f[:, :], -float(R), part_f[:, 0:1], ALU.mult,
                                    ALU.add).then_inc(setup_step, 1)
            nc.vector.tensor_scalar(lang_bias[0:NB, :], expert_f[0:NB, :], ids1_f[:, 0:1], LANG_BIAS, ALU.is_equal,
                                    ALU.mult).then_inc(lang_ready, 1)
            dve.wait_ge(setup_step, 6)
            nc.vector.tensor_single_scalar(below[:, :], mask0[:, :], float(R) - 0.5, op=ALU.is_lt).then_inc(setup_step, 1)
            dve.wait_ge(setup_step, 7)
            nc.vector.scalar_tensor_tensor(out=mask0[:, :], in0=mask0[:, :], scalar=-0.5, in1=below[:, :], op0=ALU.is_gt,
                                           op1=ALU.mult).then_inc(setup_step, 1)
            dve.wait_ge(setup_step, 8)
            H_half(0)
            f0W_low(0)
            low("c0A", c0A_split[1][:, :, :, :], c0A_sb[:, :, :, :].rearrange("p e j r -> p j e r"), c0A_split[0][:, :, :, :])
            for j in range(1, C):
                f0W_low(j)
            H_low(0)
            low("M1", M1[1][:, :], wide[1][:, :], M1[0][:, :])
            x_tile(4)
            x_tile(5)
            dve.wait_ge(consts_made, 4)
            in_turn(gate0(0), x_tiles(6, 7))
            low("f0B", f0BT[1][:, :], BT_full[:, :], f0BT[0][:, :])
            H_half(1)
            gated_low("a0", HALVES[0])
            H_low(1)
            in_turn(x1T_half(0), gate0(1))
            low("f1B", f1BT_lo[:, :], BT_full[0:ER4, :], f1BT_hi2[0:ER4, :])
            gated_low("a1", HALVES[1])
            in_turn(gate1(0))
            in_turn(x1T_half(1))
            in_turn(gate2(0))
            in_turn(gate1(1))
            mixed_low("m0", GROUPS[0])
            in_turn(gate1(2))
            in_turn(gate2(1))
            in_turn(gate2(2))
            mixed_low("m1", GROUPS[1])
            mixed_low("m2", GROUPS[2])
            dve.wait_ge(y_done, 7)
            nc.vector.tensor_copy(out_sb[:, 6, :], y_bank(6)[:, :]).then_inc(tile6_out, 1)

        @block.tensor
        def _(pe):
            def fill(name):
                k, n = fill_bank(name), fill_count(name)
                if n > 1:
                    before = FILLS[k][n - 2]
                    if before in COPIED:
                        pe.wait_ge(emptied[k], copied_count(before))
                    else:
                        pe.wait_ge(lo_ready, split_count(before))
                return tbank[fill_bank(name)]

            def done(name, ins):
                ins.then_inc(filled[fill_bank(name)], 1)

            def transposes(dst, n, src):
                for c in range(n):
                    s = src(c)
                    k, m = s.shape
                    last = nc.tensor.transpose(dst[0:m, c * k:(c + 1) * k], s, ident[0:k, 0:k])
                return last

            def split_products(dst, a, b, start, stop, a_lo=None, b_hi=None, b_lo=None):
                n = len(a)
                for c in range(n):
                    if b_hi:
                        pe.wait_ge(hi_ready, split_count(b_hi[c]))
                    nc.tensor.matmul(dst, a[c][0], b[c][0], start=start and c == 0, stop=False, skip_group_check=True)
                if a_lo:
                    pe.wait_ge(lo_ready, split_count(a_lo))
                for c in range(n):
                    nc.tensor.matmul(dst, a[c][1], b[c][0], start=False, stop=False, skip_group_check=True)
                for c in range(n):
                    if b_lo:
                        pe.wait_ge(lo_ready, split_count(b_lo[c]))
                    last = nc.tensor.matmul(dst, a[c][0], b[c][1], start=False, stop=stop and c == n - 1,
                                            skip_group_check=True)
                return last

            def part(p, *idx):
                return p[0][idx], p[1][idx]

            def x_tile(i):
                n = f"x{i}"
                done(n, transposes(fill(n), C, lambda c: x_sb[:, i, c * P:(c + 1) * P]))

            def f0W_T(j):
                n = f"fW{j}"
                done(n, transposes(fill(n), C, lambda k: o4(f0W_sb[:, k, :])[:, j, :]))

            def h0(h, tiles):
                at = (tiles[0] - HALVES[h][0]) * P
                newest = [f"x{tiles[-1]}"] * C
                last = split_products(wide[0][:, at:at + len(tiles) * P], [part(c0BT, slice(None), c) for c in range(C)],
                                      [part(xTs, slice(None), c, tokens(tiles)) for c in range(C)], True, True,
                                      "c0B", newest, newest)
                if tiles[-1] == HALVES[h][-1]:
                    last.then_inc(h0_done, 1)

            def warm(n):
                for _ in range(n):
                    nc.tensor.transpose(wide[1][:, 0:P], ident[:, :], ident[:, :])

            def log0(h):
                pe.wait_ge(H_ready, h + 1)
                for i in HALVES[h]:
                    o = (i % TPB) * N0
                    last = nc.tensor.matmul(cbank[i // TPB][:, o:o + N0], H_full[:, i * P:(i + 1) * P], M1_narrow[:, :],
                                            start=True, stop=True, skip_group_check=True)
                last.then_inc(log0_done, 1)

            def gated_T(name, n, tiles, rows=ER):
                pe.wait_ge(gated_ready, n)
                done(name, transposes(fill(name), len(tiles), lambda k: gated[:, tiles[k], 0:rows]))

            def x1T(h, chunks):
                s = tokens(HALVES[h])
                pe.wait_ge(lo_ready, split_count(f"H{h}"))
                for j in chunks:
                    b = x1T_bank(h, j)[:, :]
                    w = slice(j * P, (j + 1) * P)
                    split_products(b, [part(M1, slice(None), w)], [part(H, slice(None), s)], True, False)
                    split_products(b, [part(f0BT, slice(None), w)], [part(gatedT, slice(None), s)], False, True,
                                   None, [f"a{h}"], [f"a{h}"]).then_inc(x1T_done, 1)

            def log1_part(tiles, chunks):
                h, last_bank = tiles[0] // HALF, tiles[-1] % HALF // TPB
                for c in chunks:
                    pe.wait_ge(x1T_ready, h * C + max(c, last_bank) + 1)
                    for i in tiles:
                        o = (i % TPB) * NQ
                        nc.tensor.matmul(cbank[i // TPB][:, o:o + NQ], xT[:, c, i * P:(i + 1) * P], Q[:, c, :],
                                         start=(c == 0 and i % TPB == 0), stop=False, skip_group_check=True)

            def log1_bias(tiles):
                for i in tiles:
                    o = (i % TPB) * NQ + ER
                    last = nc.tensor.matmul(cbank[i // TPB][:, o:o + E],
                                            batch_of_token[:, i * (P // S):(i + 1) * (P // S), :].rearrange("p b s -> p (b s)"),
                                            lang_bias[:, :], start=False, stop=True, skip_group_check=True)
                last.then_inc(log1_done, 1)

            def mid(g):
                pe.wait_ge(emptied[fill_bank(f"b{g}")], copied_count(f"b{g}"))
                for i in GROUPS[g]:
                    o = (i % TPB) * NQ + ER + E
                    last = nc.tensor.matmul(cbank[i // TPB][:, o:o + NPP], gatedT1[:, i * P:(i + 1) * P], c1BP[:, :],
                                            start=False, stop=True, skip_group_check=True)
                last.then_inc(mid_done, 1)

            def y_back(tiles):
                for i in tiles:
                    if i > 4:
                        pe.wait_ge(y_out, i - 4)
                    for c in range(C):
                        nc.tensor.matmul(y_bank(i)[:, c * P:(c + 1) * P], xT[:, c, i * P:(i + 1) * P], ident[:, :],
                                         is_transpose=True, start=(c == 0), stop=False, skip_group_check=True)

            def y(g, tiles):
                pe.wait_ge(lo_ready, split_count(f"m{g}"))
                for i in tiles:
                    b = y_bank(i)
                    s = slice(i * P, (i + 1) * P)
                    nc.tensor.matmul(b[:, :], mixedT[:, s], f1BT_hi2[:, :], start=False, stop=False, skip_group_check=True)
                    nc.tensor.matmul(b[:, :], mixedT[0:ER4, s], f1BT_lo[:, :], start=False, stop=True,
                                     skip_group_check=True).then_inc(y_done, 1)

            pe.wait_ge(consts_made, 1)
            warm(8)
            pe.wait_ge(ld["c0B"], 16)
            done("c0B", transposes(fill("c0B"), C, lambda c: c0B_sb[:, c * P:(c + 1) * P]))
            for i in range(HALF):
                if i == 0:
                    warm(3)
                if i % 2 == 0:
                    pe.wait_ge(ld[f"x{i}{i + 1}"], 16)
                x_tile(i)
            h0(0, range(0, TPB))
            h0(0, range(TPB, HALF))
            pe.wait_ge(ld["f0W"], 16)
            for j in range(C):
                f0W_T(j)
            pe.wait_ge(ld["f0A"], 16)
            done("f0A", transposes(fill("f0A"), C, lambda j: o4(f0A_sb[:, :])[:, j, :]))
            pe.wait_ge(ld["router"], 16)
            pe.wait_ge(ld["small"], 32)
            pe.wait_ge(ld["pp"], 32)
            b = fill("small")
            transposes(b, C, lambda j: o4(f0Wr_sb[:, :])[:, j, :])
            transposes(b[:, WR_AT:B_AT], C, lambda c: c1Wr_sb[:, c * P:(c + 1) * P])
            nc.tensor.transpose(b[:, B_AT:PP_AT], f0b_sb[:, :], ident[0:C, 0:C])
            done("small", transposes(b[:, PP_AT:PP_AT + C * NPP], C, lambda j: o4(pp_sb[:, :])[:, j, :]))
            chunks = [f"fW{j}" for j in range(C)]
            pe.wait_ge(hi_ready, split_count("c0A"))
            last = split_products(wide[1][:, :], [(er(c0A_split[0], j), er(c0A_split[1], j)) for j in range(C)],
                                  [part(f0WT, slice(None), j) for j in range(C)], True, True, "c0A", chunks, chunks)
            last.then_inc(m1_wide_done, 1)
            pe.wait_ge(repacked, 1)
            for n in ("f0A", "small"):
                pe.wait_ge(emptied[fill_bank(n)], copied_count(n))
            for j in range(C):
                last = nc.tensor.matmul(cbank[3][:, 0:N0], er(c0A_er, j), f0T_narrow[:, j, :], start=(j == 0), stop=(j == C - 1))
            last.then_inc(m1_narrow_done, 1)
            pe.wait_ge(ld["xh1"], 16)
            x_tile(4)
            x_tile(5)
            pe.wait_ge(narrow_ready, 1)
            log0(0)
            x_tile(6)
            x_tile(7)
            pe.wait_ge(ld["c1W"], 16)
            pe.wait_ge(lo_ready, split_count("M1"))
            for c in range(C):
                for j in range(C):
                    last = nc.tensor.matmul(wide[1][:, c * NPP:(c + 1) * NPP], c1W_sb[:, j, c * P:(c + 1) * P], ppT[:, j, :],
                                            start=(j == 0), stop=(j == C - 1), skip_group_check=True)
            last.then_inc(qp_done, 1)
            pe.wait_ge(repacked, 2)
            done("f0B", transposes(fill("f0B"), C, lambda j: er(f0B_er, j)))
            h0(1, HALVES[1])
            gated_T("a0", 1, HALVES[0])
            pe.wait_ge(ld["c1A"], 16)
            done("c1A", transposes(fill("c1A"), C, lambda c: c1A_sb[:, c * P:(c + 1) * P]))
            pe.wait_ge(H_ready, 2)
            pe.wait_ge(repacked, 3)
            for j in range(C):
                last = nc.tensor.matmul(wide[0][:, 0:NPP], er(c1B_er, j), ppT[:, j, :], start=(j == 0), stop=(j == C - 1))
            last.then_inc(bp_done, 1)
            log0(1)
            x1T(0, [0, 1])
            pe.wait_ge(repacked, 4)
            done("f1B", transposes(fill("f1B"), C, lambda j: er(f1B_er, j)))
            pe.wait_ge(qp_ready, 1)
            pe.wait_ge(bp_ready, 1)
            x1T(0, [2, 3])
            log1_part(GROUPS[0], [0, 1, 2])
            gated_T("a1", 2, HALVES[1])
            log1_part(GROUPS[0], [3])
            pe.wait_ge(consts_made, 5)
            pe.wait_ge(lang_ready, 1)
            log1_bias(GROUPS[0])
            x1T(1, [0, 1, 2])
            gated_T("b0", 3, GROUPS[0])
            x1T(1, [3])
            mid(0)
            log1_part(GROUPS[1], range(C))
            log1_bias(GROUPS[1])
            gated_T("m0", 4, GROUPS[0], ER4)
            log1_part(GROUPS[2], range(C))
            log1_bias(GROUPS[2])
            gated_T("b1", 5, GROUPS[1])
            y_back([0])
            mid(1)
            y_back([1, 2, 3])
            y(0, [0])
            gated_T("b2", 6, GROUPS[2])
            y(0, [1, 2])
            mid(2)
            y(0, [3])
            gated_T("m1", 7, GROUPS[1], ER4)
            y_back([4, 5, 6, 7])
            gated_T("m2", 8, GROUPS[2], ER4)
            y(1, GROUPS[1])
            y(2, GROUPS[2])


_INS = ['x', 'itok_B_3_7', 'itok_B_0_7', 'L0_cond_A', 'L0_cond_B', 'L0_ffn_W_base', 'L0_ffn_b_base', 'L0_ffn_W_router',
        'L0_ffn_A', 'L0_ffn_B', 'L1_cond_W', 'L1_cond_Wr', 'L1_cond_A', 'L1_cond_B', 'L1_ffn_A', 'L1_ffn_B', 'L1_ffn_Wr']
_OUTS = [((32, 32, 512), 'float32')]


def kernel(**inputs):
    import numpy as _np
    import concourse.bacc as _bacc
    from concourse import mybir as _mybir
    from concourse.bass_utils import run_bass_kernel_spmd as _run

    nc = _bacc.Bacc("TRN2", target_bir_lowering=False, num_devices=1)
    arrays, args = {}, []
    for name in _INS:
        a = _np.ascontiguousarray(inputs[name])
        arrays[f"in_{name}_dram"] = a
        args.append(nc.dram_tensor(f"in_{name}_dram", a.shape, _mybir.dt.from_np(a.dtype), kind="ExternalInput").ap())
    for i, (shape, dtype) in enumerate(_OUTS):
        dt = _mybir.dt.from_np(_np.dtype(dtype))
        args.append(nc.dram_tensor(f"out_{i}_dram", shape, dt, kind="ExternalOutput").ap())
    adaln_ffn_two_layers(nc, *args)
    r = _run(nc, [arrays], core_ids=[0])
    got = tuple(r.results[0][f"out_{i}_dram"] for i in range(len(_OUTS)))
    return got[0]
```
